# Optimizing a Trainium2 kernel written in Bass

```python
import numpy as np
import jax
import jax.numpy as jnp

def _softmax(x, axis=-1):
    return jax.nn.softmax(x, axis=axis)

def _gelu(x):
    return jax.nn.gelu(x, approximate=True)

def _silu(x):
    return jax.nn.silu(x)

def _sigmoid(x):
    return jax.nn.sigmoid(x)

def _layernorm(x, axis=-1, eps=1e-05):
    m = jnp.mean(x, axis=axis, keepdims=True)
    v = jnp.var(x, axis=axis, keepdims=True)
    return (x - m) / jnp.sqrt(v + eps)

def _scatter_add(tgt, idx, src, axis=0):
    return tgt.at[idx].add(src)

def _segment_sum(src, seg, n):
    return jax.ops.segment_sum(src, seg, n)
kernel_name = 'mk_gnn_preln_d2_gnn_r8_6cdd21'

def setup_inputs(seed: int=0):
    np.random.seed(seed)
    _w = jnp.asarray

    def _rec_inputs():
        import jax
        import jax.numpy as jnp
        _gk = jax.random.key(seed)
        x = -0.000202 + 1 * jax.random.normal(jax.random.fold_in(_gk, 1), (6250, 128), jnp.float32)
        _s = jax.random.randint(jax.random.fold_in(_gk, 2), (100000,), 0, 6250, jnp.int32)
        _d = jax.random.randint(jax.random.fold_in(_gk, 3), (100000,), 0, 6250, jnp.int32)
        _loop = jnp.arange(6250, dtype=jnp.int32)
        src = jnp.concatenate([_s, _d, _loop])
        dst = jnp.concatenate([_d, _s, _loop])
        _o = jnp.argsort(dst, stable=True)
        src = src[_o]
        dst = dst[_o]
        return (x, src, dst)
    x, src, dst = _rec_inputs()

    def _L0_gnn_setup():
        import jax, jax.numpy as jnp
        import numpy as np
        N, D, E, EDIM, HID = (6250, 128, 62500, 64, 128)
        LN_EPS = 1e-05

        def _layernorm(x, g, b):
            m = jnp.mean(x, axis=-1, keepdims=True)
            v = jnp.mean(jnp.square(x - m), axis=-1, keepdims=True)
            return (x - m) * jax.lax.rsqrt(v + LN_EPS) * g + b

        def _gcn(x, W, b, row, col, ew):
            xw = x @ W
            deg = jax.ops.segment_sum(ew, col, num_segments=N) + 1.0
            dinv = jax.lax.rsqrt(deg)
            norm = dinv[row] * ew * dinv[col]
            agg = jax.ops.segment_sum(norm[:, None] * xw[row], col, num_segments=N)
            agg = agg + (dinv * dinv)[:, None] * xw
            return agg + b
        key = jax.random.key(seed)
        ks = jax.random.split(key, 24)

        def lin(k, fi, fo):
            return jax.random.normal(k, (fi, fo), jnp.float32) / np.sqrt(fi)
        return {'x': jax.random.normal(ks[0], (N, D), jnp.float32), 'edge_index': jax.random.randint(ks[1], (2, E), 0, N, jnp.int32), 'W1': lin(ks[2], D, D), 'b1': jnp.zeros((D,), jnp.float32), 'W2': lin(ks[3], D, D), 'b2': jnp.zeros((D,), jnp.float32), 'ln1_g': jnp.ones((D,), jnp.float32), 'ln1_b': jnp.zeros((D,), jnp.float32), 'ln2_g': jnp.ones((D,), jnp.float32), 'ln2_b': jnp.zeros((D,), jnp.float32), 'ei_w1': lin(ks[4], 2 * D, EDIM), 'ei_b1': jnp.zeros((EDIM,), jnp.float32), 'ei_w2': lin(ks[5], EDIM, EDIM), 'ei_b2': jnp.zeros((EDIM,), jnp.float32), 'eu_w1': lin(ks[6], 2 * D + EDIM, HID), 'eu_b1': jnp.zeros((HID,), jnp.float32), 'eu_w2': lin(ks[7], HID, EDIM), 'eu_b2': jnp.zeros((EDIM,), jnp.float32), 'lne_g': jnp.ones((EDIM,), jnp.float32), 'lne_b': jnp.zeros((EDIM,), jnp.float32), 'ew_w': lin(ks[8], EDIM, 1), 'ew_b': jnp.zeros((1,), jnp.float32)}
    _L0_gnn_all = _L0_gnn_setup()
    _L0_gnn_in = {k: v for k, v in _L0_gnn_all.items() if k in ('W1', 'b1', 'W2', 'b2', 'ln1_g', 'ln1_b', 'ln2_g', 'ln2_b', 'ei_w1', 'ei_b1', 'ei_w2', 'ei_b2', 'eu_w1', 'eu_b1', 'eu_w2', 'eu_b2', 'lne_g', 'lne_b', 'ew_w', 'ew_b')}
    del _L0_gnn_all

    def _L1_gnn_setup():
        import jax, jax.numpy as jnp
        import numpy as np
        N_NODES = 6250
        N_EDGES = 75000
        IN_FEATS = 128
        OUT_FEATS = 128
        EPS = 1e-12
        key = jax.random.key(seed)
        k_h, k_w, k_b, k_s, k_d = jax.random.split(key, 5)
        h = jax.random.normal(k_h, (N_NODES, IN_FEATS), dtype=jnp.float32)
        W = jax.random.normal(k_w, (2 * IN_FEATS, OUT_FEATS), dtype=jnp.float32) * 0.05
        b = jax.random.normal(k_b, (OUT_FEATS,), dtype=jnp.float32) * 0.05
        src = jax.random.randint(k_s, (N_EDGES,), 0, N_NODES, dtype=jnp.int32)
        dst = jax.random.randint(k_d, (N_EDGES,), 0, N_NODES, dtype=jnp.int32)
        return {'h': h, 'W': W, 'b': b, 'src': src, 'dst': dst}
    _L1_gnn_all = _L1_gnn_setup()
    _L1_gnn_in = {k: v for k, v in _L1_gnn_all.items() if k in ('W', 'b')}
    del _L1_gnn_all
    return {'x': x, 'src': src, 'dst': dst, 'L0_gnn_W1': _L0_gnn_in['W1'], 'L0_gnn_b1': _L0_gnn_in['b1'], 'L0_gnn_W2': _L0_gnn_in['W2'], 'L0_gnn_b2': _L0_gnn_in['b2'], 'L0_gnn_ln1_g': _L0_gnn_in['ln1_g'], 'L0_gnn_ln1_b': _L0_gnn_in['ln1_b'], 'L0_gnn_ln2_g': _L0_gnn_in['ln2_g'], 'L0_gnn_ln2_b': _L0_gnn_in['ln2_b'], 'L0_gnn_ei_w1': _L0_gnn_in['ei_w1'], 'L0_gnn_ei_b1': _L0_gnn_in['ei_b1'], 'L0_gnn_ei_w2': _L0_gnn_in['ei_w2'], 'L0_gnn_ei_b2': _L0_gnn_in['ei_b2'], 'L0_gnn_eu_w1': _L0_gnn_in['eu_w1'], 'L0_gnn_eu_b1': _L0_gnn_in['eu_b1'], 'L0_gnn_eu_w2': _L0_gnn_in['eu_w2'], 'L0_gnn_eu_b2': _L0_gnn_in['eu_b2'], 'L0_gnn_lne_g': _L0_gnn_in['lne_g'], 'L0_gnn_lne_b': _L0_gnn_in['lne_b'], 'L0_gnn_ew_w': _L0_gnn_in['ew_w'], 'L0_gnn_ew_b': _L0_gnn_in['ew_b'], 'L1_gnn_W': _L1_gnn_in['W'], 'L1_gnn_b': _L1_gnn_in['b']}

def reference(x, src, dst, L0_gnn_W1, L0_gnn_b1, L0_gnn_W2, L0_gnn_b2, L0_gnn_ln1_g, L0_gnn_ln1_b, L0_gnn_ln2_g, L0_gnn_ln2_b, L0_gnn_ei_w1, L0_gnn_ei_b1, L0_gnn_ei_w2, L0_gnn_ei_b2, L0_gnn_eu_w1, L0_gnn_eu_b1, L0_gnn_eu_w2, L0_gnn_eu_b2, L0_gnn_lne_g, L0_gnn_lne_b, L0_gnn_ew_w, L0_gnn_ew_b, L1_gnn_W, L1_gnn_b):
    import jax
    import jax.numpy as jnp

    def _L0_gnn_ref(x, edge_index, W1, b1, W2, b2, ln1_g, ln1_b, ln2_g, ln2_b, ei_w1, ei_b1, ei_w2, ei_b2, eu_w1, eu_b1, eu_w2, eu_b2, lne_g, lne_b, ew_w, ew_b):
        import jax, jax.numpy as jnp
        import numpy as np
        N, D, E, EDIM, HID = (6250, 128, 62500, 64, 128)
        LN_EPS = 1e-05

        def _layernorm(x, g, b):
            m = jnp.mean(x, axis=-1, keepdims=True)
            v = jnp.mean(jnp.square(x - m), axis=-1, keepdims=True)
            return (x - m) * jax.lax.rsqrt(v + LN_EPS) * g + b

        def _gcn(x, W, b, row, col, ew):
            xw = x @ W
            deg = jax.ops.segment_sum(ew, col, num_segments=N) + 1.0
            dinv = jax.lax.rsqrt(deg)
            norm = dinv[row] * ew * dinv[col]
            agg = jax.ops.segment_sum(norm[:, None] * xw[row], col, num_segments=N)
            agg = agg + (dinv * dinv)[:, None] * xw
            return agg + b
        row, col = (edge_index[0], edge_index[1])
        e_in = jnp.concatenate([x[row], x[col]], axis=-1)
        ef = jax.nn.relu(e_in @ ei_w1 + ei_b1) @ ei_w2 + ei_b2
        ew = jax.nn.sigmoid(ef @ ew_w + ew_b)[:, 0]
        out1 = _layernorm(jax.nn.gelu(_gcn(x, W1, b1, row, col, ew), approximate=False), ln1_g, ln1_b)
        cat = jnp.concatenate([out1[row], out1[col], ef], axis=-1)
        ef = _layernorm(ef + (jax.nn.relu(cat @ eu_w1 + eu_b1) @ eu_w2 + eu_b2), lne_g, lne_b)
        ew = jax.nn.sigmoid(ef @ ew_w + ew_b)[:, 0]
        out2 = _layernorm(jax.nn.gelu(_gcn(out1, W2, b2, row, col, ew), approximate=False), ln2_g, ln2_b)
        return out2

    def _L1_gnn_ref(h, W, b, src, dst):
        import jax, jax.numpy as jnp
        import numpy as np
        N_NODES = 6250
        N_EDGES = 75000
        IN_FEATS = 128
        OUT_FEATS = 128
        EPS = 1e-12
        n = h.shape[0]
        msg_sum = jax.ops.segment_sum(h[src], dst, num_segments=n)
        deg = jax.ops.segment_sum(jnp.ones_like(src, dtype=h.dtype), dst, num_segments=n)
        c = msg_sum / jnp.maximum(deg, 1.0)[:, None]
        bundle = jnp.concatenate([h, c], axis=1) @ W + b
        norm = jnp.maximum(jnp.linalg.norm(bundle, axis=1, keepdims=True), EPS)
        return jax.nn.relu(bundle / norm)
    edge_index = jnp.stack([src, dst])
    h = jnp.maximum(_layernorm(x, axis=-1), 0.0)
    x = x + _L0_gnn_ref(h, edge_index, L0_gnn_W1, L0_gnn_b1, L0_gnn_W2, L0_gnn_b2, L0_gnn_ln1_g, L0_gnn_ln1_b, L0_gnn_ln2_g, L0_gnn_ln2_b, L0_gnn_ei_w1, L0_gnn_ei_b1, L0_gnn_ei_w2, L0_gnn_ei_b2, L0_gnn_eu_w1, L0_gnn_eu_b1, L0_gnn_eu_w2, L0_gnn_eu_b2, L0_gnn_lne_g, L0_gnn_lne_b, L0_gnn_ew_w, L0_gnn_ew_b)
    h = jnp.maximum(_layernorm(x, axis=-1), 0.0)
    x = x + _L1_gnn_ref(h, L1_gnn_W, L1_gnn_b, src, dst)
    return x

_drawn_inputs = setup_inputs


def setup_inputs(seed=0):
    import zlib

    import numpy as np

    out = dict(_drawn_inputs(seed))
    spreads = {'L0_gnn_b1': (0.0, 0.1),
     'L0_gnn_b2': (0.0, 0.1),
     'L0_gnn_ln1_g': (1.0, 0.2),
     'L0_gnn_ln1_b': (0.0, 0.1),
     'L0_gnn_ln2_g': (1.0, 0.2),
     'L0_gnn_ln2_b': (0.0, 0.1),
     'L0_gnn_ei_b1': (0.0, 0.8),
     'L0_gnn_ei_b2': (0.0, 0.8),
     'L0_gnn_eu_b1': (0.0, 0.8),
     'L0_gnn_eu_b2': (0.0, 0.8),
     'L0_gnn_lne_g': (1.0, 0.6),
     'L0_gnn_lne_b': (0.0, 0.8)}
    factors = {'L0_gnn_ei_w1': 3.021,
     'L0_gnn_ei_w2': 3.189,
     'L0_gnn_eu_w1': 7.071,
     'L0_gnn_eu_w2': 7.791,
     'L0_gnn_ew_w': 2.731,
     'L1_gnn_b': 8.0}
    for name, (base, spread) in spreads.items():
        noise = np.random.default_rng([zlib.crc32(name.encode()), seed]).standard_normal(out[name].shape)
        drawn = base * np.exp(spread * noise) if base else spread * noise
        out[name] = jnp.asarray(drawn.astype(out[name].dtype))
    for name, factor in factors.items():
        out[name] = (out[name] * factor).astype(out[name].dtype)
    return out
```

```python
import concourse.bass as bass
from concourse import mybir
from contextlib import ExitStack

F32 = mybir.dt.float32
I32 = mybir.dt.int32
ALU = mybir.AluOpType
ACT = mybir.ActivationFunctionType
AXX = mybir.AxisListType.X
ds = bass.ds


def build(nc, x, src, dst, W1, b1, W2, b2, ln1_g, ln1_b, ln2_g, ln2_b, ei_w1, ei_b1, ei_w2, ei_b2,
          eu_w1, eu_b1, eu_w2, eu_b2, lne_g, lne_b, ew_w, ew_b, L1_W, L1_b, out):
    P = 128
    N, D = x.shape
    E = src.shape[0]
    NT = -(-N // P)
    NPAD = NT * P
    FULL = N // NT
    REST = N - FULL * NT
    SUB = 4
    GE = SUB * P
    U = 4
    G = -(-E // (GE * U)) * U
    STEPS = G // U
    EPAD = G * GE
    GP = STEPS
    WIN = 64
    MAXR = N // WIN + 1
    NALL = -(-(N + MAXR * WIN) // P) * P
    ED = ei_w2.shape[0]
    PR = ED + D
    K = G * SUB
    CREDIT = 4
    LN_EPS = 1e-5

    def done(i):
        return i + 1 + CREDIT

    ctx = ExitStack()
    with ctx:
        sb = lambda n, s, d=F32: ctx.enter_context(nc.sbuf_tensor(n, s, d))
        sem = lambda n: ctx.enter_context(nc.semaphore(n))
        dram = lambda n, s, d=F32: nc.dram_tensor(n, s, d, kind="Internal").ap()

        src_pad = dram("src_pad", (EPAD,), I32)
        dst_pad = dram("dst_pad", (EPAD,), I32)
        rel_d = dram("rel_d", (EPAD,))
        span_d = dram("span_d", (G,), I32)
        base_d = dram("base_d", (G,), I32)
        deg_d = dram("deg_d", (2, NPAD))
        tab_p = dram("tab_p", (NPAD, ED))
        tab_q = dram("tab_q", (NALL, ED))
        tab_pr = dram("tab_pr", (NPAD, PR))
        tab_qs = dram("tab_qs", (NALL, PR))
        tab_h = dram("tab_h", (NPAD, D))

        x_sb = sb("x_sb", [P, NT, D])
        h_sb = sb("h_sb", [P, NT, D])
        area = sb("area", [P, NT * D])
        big = area[:, :].rearrange("p (t d) -> p t d", d=D)
        rows_gat = area[:, 0:U * SUB * PR].rearrange("p (u j f) -> p u j f", u=U, j=SUB)
        o1 = U * SUB * PR
        rel_row = area[0:WIN, o1:o1 + U * GE].rearrange("p (u e) -> p u e", u=U)
        o2 = o1 + U * GE
        hotT = area[0:WIN, o2:o2 + 2 * GE].rearrange("p (s e) -> p s e", s=2)
        assert o2 + 2 * GE <= NT * D
        acc = sb("acc", [P, NALL])
        stats = acc[:, 0:K * 6].rearrange("p (k s) -> p k s", s=6)
        rel = sb("rel", [P, K])
        ew2 = sb("ew2", [P, K, 2])
        rawz = sb("rawz", [P, K])
        tmpa = sb("tmpa", [P, K])
        tmpb = sb("tmpb", [P, K])
        idx = sb("idx", [P, 2, 2, SUB], I32)
        win = sb("win", [WIN, U, PR])
        hot = sb("hot", [P, 2, SUB, WIN])
        wts = sb("wts", [P, 2, SUB, 2])
        stage = sb("stage", [P, 2, P])
        tT = sb("tT", [ED + 1, 2, GE])
        uT = sb("uT", [P, 2, GE])
        base_sb = sb("base_sb", [1, G], I32)
        iota_row0 = sb("iota_row0", [P, WIN])
        iota_row = sb("iota_row", [P, WIN])
        iota_i = sb("iota_i", [P, WIN], I32)
        iota_c = sb("iota_c", [P, 1], I32)
        iota_col0 = sb("iota_col0", [P, 1])
        iota_col = sb("iota_col", [P, 1])
        ident = sb("ident", [P, P])
        hT = sb("hT", [P, 2, P])
        rounds_sb = sb("rounds_sb", [1, 4], I32)
        s1 = sb("s1", [P, NT])
        s2 = sb("s2", [P, NT])
        dinv = sb("dinv", [P, NT])
        cinv = sb("cinv", [P, NT])
        w_pq = sb("w_pq", [P, 2 * ED])
        w1 = sb("w1", [P, D])
        w2 = sb("w2", [P, D])
        u1 = sb("u1", [P, D])
        u2 = sb("u2", [P, D])
        u3 = sb("u3", [ED, D])
        l1a = sb("l1a", [P, D])
        l1b = sb("l1b", [P, D])
        rowv = sb("rowv", [P, 7, D])
        eib1 = sb("eib1", [ED, 1])
        eub1 = sb("eub1", [P, 1])
        wz = sb("wz", [ED + 1, ED + 1])
        wv = sb("wv", [P, ED + 1])
        wtu = sb("wtu", [ED + 1, D])
        wl = sb("wl", [ED + 1, 1])
        eiw = sb("eiw", [ED + 1, ED])
        eiwz = sb("eiwz", [ED + 1, ED])
        eub2 = sb("eub2", [ED + 1, ED])
        eiwT = sb("eiwT", [ED, ED + 1])
        eiwzT = sb("eiwzT", [ED, ED + 1])
        euwT = sb("euwT", [ED, P])
        lvec = sb("lvec", [ED, 4])
        ewb = sb("ewb", [P, 1])
        sgw = sb("sgw", [P, 2])
        ones = sb("ones", [ED, P])
        prod = sb("prod", [ED, 2])
        eps_ln = sb("eps_ln", [P, 1])

        pb = lambda n: ctx.enter_context(nc.psum_tensor(n, [P, 512], F32))
        pt = [pb("pt0"), pb("pt1")]
        pu = [pb("pu0"), pb("pu1")]
        pz = [pb("pz0"), pb("pz1")]

        s_load = sem("loaded")
        s_store = sem("stored")
        s_pool = sem("pool_step")
        s_dve = sem("dve_step")
        s_act = sem("act_step")
        s_pe = sem("pe_step")
        s_idx = [sem(f"idx_in{h}") for h in range(2)]
        s_gat = [[sem(f"rows_in{u}_{j}") for j in range(SUB)] for u in range(U)]
        s_win = [sem(f"window_in{u}") for u in range(U)]
        s_hotT = sem("hotT_ready")
        s_hot = sem("hot_ready")
        s_t = sem("t_done")
        s_relu = sem("t_relu_done")
        s_u = sem("u_done")
        s_urelu = sem("u_relu_done")
        s_z = sem("z_done")
        s_zcp = sem("z_copied")
        s_sum = sem("sum_done")
        s_acc = sem("acc_added")
        s_stage = sem("tile_staged")
        all_sems = [s_load, s_store, s_pool, s_dve, s_act, s_pe, *s_idx, *sum(s_gat, []), *s_win, s_hotT, s_hot, s_t,
                    s_relu, s_u, s_urelu, s_z, s_zcp, s_sum, s_acc, s_stage]

        def end_stage():
            nc.gpsimd.dma_reset()
            for s in all_sems:
                nc.gpsimd.sem_clear(s)
            nc.all_engine_barrier()

        def chain(eng, sm):
            n = [0]

            def link(ins):
                n[0] += 1
                ins.then_inc(sm, 1)
                eng.wait_ge(sm, n[0])
            return link

        with nc.Block() as block:
            @block.sync
            def _(sp):
                def load(d_, s_):
                    sp.dma_start(d_, s_).then_inc(s_load, 16)
                sp.wait_ge(s_dve, 1)
                load(x_sb[0:FULL, :, :], x[0:FULL * NT, :].rearrange("(p t) d -> p t d", t=NT))
                load(x_sb[FULL:FULL + 1, 0:REST, :], x[FULL * NT:N, :].rearrange("(p t) d -> p t d", p=1))
                load(src_pad[0:E], src)
                load(dst_pad[0:E], dst)
                col = lambda v: v.rearrange("(p o) -> p o", o=1)
                load(w_pq[:, 0:ED], ei_w1[0:D, :])
                load(w_pq[:, ED:2 * ED], ei_w1[D:2 * D, :])
                load(w1[:, :], W1)
                load(w2[:, :], W2)
                load(u1[:, :], eu_w1[0:D, :])
                load(u2[:, :], eu_w1[D:2 * D, :])
                load(u3[:, :], eu_w1[2 * D:2 * D + ED, :])
                load(l1a[:, :], L1_W[0:D, :])
                load(l1b[:, :], L1_W[D:2 * D, :])
                for k, v in enumerate((b1, b2, ln1_g, ln1_b, ln2_g, ln2_b, L1_b)):
                    load(rowv[:, k, :], v.rearrange("(o d) -> o d", o=1).broadcast_to([P, D]))
                load(eib1[:, :], col(ei_b1))
                load(eub1[:, :], col(eu_b1))
                load(eiw[0:ED, :], ei_w2)
                load(eiw[ED:ED + 1, :], ei_b2.rearrange("(o d) -> o d", o=1))
                load(eub2[ED:ED + 1, :], eu_b2.rearrange("(o d) -> o d", o=1))
                load(wv[:, 0:ED], eu_w2)
                load(lvec[:, 0:1], col(lne_g))
                load(lvec[:, 1:2], col(lne_b))
                load(lvec[:, 2:3], ew_w)
                load(ewb[:, :], ew_b.rearrange("(o d) -> o d", o=1).broadcast_to([P, 1]))
                nload = 3 + 9 + 1 + 7 + 10
                sp.wait_ge(s_dve, 3)
                PADE = EPAD - E
                load(src_pad[E:EPAD].rearrange("(o e) -> o e", o=1), rel[0:1, 0:PADE].bitcast(I32))
                load(dst_pad[E:EPAD].rearrange("(o e) -> o e", o=1), rawz[0:1, 0:PADE].bitcast(I32))
                sp.wait_ge(s_dve, 4)
                PASTN = (NALL - NPAD) // P
                sp.dma_start(tab_q[NPAD:NALL, :].rearrange("(p t) d -> p (t d)", p=P),
                             acc[:, 0:PASTN * ED]).then_inc(s_store, 16)
                sp.dma_start(tab_qs[NPAD:NALL, :].rearrange("(p t) d -> p (t d)", p=P),
                             acc[:, 0:PASTN * PR]).then_inc(s_store, 16)
                sp.wait_ge(s_load, 16 * (nload + 2))
                sp.wait_ge(s_store, 32)

            @block.vector
            def _(dve):
                nc.vector.memset(x_sb[:, :, :][96:P], 0.0).then_inc(s_dve, 1)
                nc.vector.memset(rel[0:1, :].bitcast(I32), 0).then_inc(s_dve, 1)
                nc.vector.memset(rawz[0:1, :].bitcast(I32), N).then_inc(s_dve, 1)
                nc.vector.memset(acc[:, :], 0.0).then_inc(s_dve, 1)
                nc.vector.memset(tT[ED:ED + 1, :, :], 1.0)
                nc.vector.memset(ew2[:, :, 1:2], 1.0)
                nc.vector.memset(ones[:, :], 1.0)
                nc.vector.memset(eps_ln[:, :], LN_EPS)
                nc.vector.memset(eub2[0:ED, :], 0.0)
                nc.vector.memset(win[:, :, :], 0.0)
                dve.wait_ge(s_pool, 4)
                nc.vector.tensor_copy(iota_row0[:, :], iota_i[:, :])
                nc.vector.tensor_copy(iota_col0[:, :], iota_c[:, :])

            @block.gpsimd
            def _(pool):
                nc.gpsimd.memset(ident[:, :], 0.0).then_inc(s_pool, 1)
                nc.gpsimd.iota(iota_i[:, :], pattern=[[1, WIN]], base=0, channel_multiplier=0).then_inc(s_pool, 1)
                nc.gpsimd.iota(iota_c[:, :], pattern=[[0, 1]], base=0, channel_multiplier=1).then_inc(s_pool, 1)
                pool.wait_ge(s_pool, 3)
                nc.gpsimd.affine_select(out=ident[:, :], in_=ident[:, :], compare_op=ALU.not_equal, fill=1.0,
                                        base=0, pattern=[[-1, P]], channel_multiplier=1).then_inc(s_pool, 1)
        end_stage()

        gdst_i = area[0:GP, 0:U * GE].bitcast(I32)
        gdst = area[0:GP, U * GE:2 * U * GE]
        gmin = s1[0:GP, 0:U]
        gmax = s1[0:GP, U:2 * U]
        gint = s2[0:GP, 0:2 * U].bitcast(I32)
        with nc.Block() as block:
            @block.sync
            def _(sp):
                sp.dma_start(gdst_i, dst_pad.rearrange("(p e) -> p e", p=GP)).then_inc(s_load, 16)
                sp.wait_ge(s_dve, 6 + U)
                sp.dma_start(rel_d.rearrange("(p e) -> p e", p=GP), gdst).then_inc(s_store, 16)
                sp.dma_start(base_d.rearrange("(p u) -> p u", p=GP), gint[:, 0:U]).then_inc(s_store, 16)
                sp.dma_start(span_d.rearrange("(p u) -> p u", p=GP), gint[:, U:2 * U]).then_inc(s_store, 16)
                sp.wait_ge(s_store, 48)
                sp.dma_start(base_sb[:, :], span_d.rearrange("(o g) -> o g", o=1)).then_inc(s_load, 16)
                sp.dma_start(rel[:, :].rearrange("p (g j) -> p g j", j=SUB),
                             rel_d.rearrange("(g p j) -> p g j", p=P, j=SUB)).then_inc(s_load, 16)
                sp.wait_ge(s_load, 48)

            @block.vector
            def _(dve):
                link = chain(dve, s_dve)
                dve.wait_ge(s_load, 16)
                link(nc.vector.tensor_copy(gdst, gdst_i))
                v = gdst.rearrange("p (u e) -> p u e", u=U)
                link(nc.vector.tensor_reduce(gmin, v, axis=AXX, op=ALU.min))
                link(nc.vector.tensor_reduce(gmax, v, axis=AXX, op=ALU.max))
                for u in range(U):
                    link(nc.vector.tensor_scalar(v[:, u, :], v[:, u, :], gmin[:, u:u + 1], None, ALU.subtract))
                link(nc.vector.tensor_tensor(gmax, gmax, gmin, ALU.subtract))
                link(nc.vector.tensor_copy(gint[:, 0:U], gmin))
                link(nc.vector.tensor_copy(gint[:, U:2 * U], gmax))
                dve.wait_ge(s_load, 48)
                n0 = 6 + U
                nc.vector.tensor_reduce(rounds_sb[:, 0:1], base_sb[:, :], axis=AXX, op=ALU.max).then_inc(s_dve, 1)
                dve.wait_ge(s_dve, n0 + 1)
                nc.vector.tensor_scalar(rounds_sb[:, 1:2], rounds_sb[:, 0:1], 6, None,
                                        ALU.arith_shift_right).then_inc(s_dve, 1)
                dve.wait_ge(s_dve, n0 + 2)
                nc.vector.tensor_scalar(rounds_sb[:, 2:3], rounds_sb[:, 1:2], 1, None, ALU.add).then_inc(s_dve, 1)
                nc.vector.tensor_tensor(eiwz[:, :], eiw[:, :], eub2[:, :], ALU.add).then_inc(s_dve, 1)
                nc.vector.tensor_tensor(lvec[:, 3:4], lvec[:, 0:1], lvec[:, 2:3], ALU.mult).then_inc(s_dve, 1)
                dve.wait_ge(s_dve, n0 + 5)
                nc.vector.tensor_copy(prod[:, 0:1], lvec[:, 3:4])
                nc.vector.tensor_tensor(prod[:, 1:2], lvec[:, 1:2], lvec[:, 2:3], ALU.mult).then_inc(s_dve, 2)
                dve.wait_ge(s_pe, 1)
                nc.vector.tensor_copy(eiwT[:, :], pt[0][0:ED, 0:ED + 1])
                nc.vector.tensor_copy(eiwzT[:, :], pt[0][0:ED, 128:128 + ED + 1])
                nc.vector.tensor_copy(euwT[:, :], pt[0][0:ED, 256:256 + P]).then_inc(s_dve, 1)
                dve.wait_ge(s_pe, 2)
                nc.vector.tensor_copy(wtu[:, :], pt[1][0:ED + 1, 0:D])
                nc.vector.tensor_copy(wl[:, :], pt[1][0:ED + 1, 128:129])
                nc.vector.tensor_copy(wz[:, ED:ED + 1], pt[1][0:ED + 1, 132:133])
                nc.vector.tensor_copy(wz[:, 0:ED], eiwz[:, :])
                nc.vector.tensor_copy(wv[:, ED:ED + 1], pt[1][:, 136:137])
                nc.vector.tensor_copy(sgw[:, :], pt[1][:, 140:142])

            @block.tensor
            def _(pe):
                n0 = 6 + U
                pe.wait_ge(s_dve, n0 + 7)
                nc.tensor.transpose(pt[0][0:ED, 0:ED + 1], eiw[:, :], ident[0:ED + 1, 0:ED + 1])
                nc.tensor.transpose(pt[0][0:ED, 128:128 + ED + 1], eiwz[:, :], ident[0:ED + 1, 0:ED + 1])
                nc.tensor.transpose(pt[0][0:ED, 256:256 + P], wv[:, 0:ED], ident[:, :]).then_inc(s_pe, 1)
                pe.wait_ge(s_dve, n0 + 8)
                mm = lambda o, l, r_: nc.tensor.matmul(o, l, r_, start=True, stop=True)
                mm(pt[1][0:ED + 1, 0:D], eiwT[:, :], u3[:, :])
                mm(pt[1][0:ED + 1, 128:129], eiwT[:, :], lvec[:, 2:3])
                mm(pt[1][0:ED + 1, 132:133], eiwzT[:, :], lvec[:, 3:4])
                mm(pt[1][:, 136:137], euwT[:, :], lvec[:, 3:4])
                mm(pt[1][:, 140:142], ones[:, :], prod[:, :]).then_inc(s_pe, 1)
        end_stage()
        rounds = nc.values_load(rounds_sb[0:1, 2:3], min_val=1, max_val=MAXR)

        def reset_windows(clear_weights=False, clear_rows=0):
            with nc.Block() as block:
                @block.sync
                def _(sp):
                    sp.dma_start(base_sb[:, :], base_d.rearrange("(o g) -> o g", o=1)).then_inc(s_load, 16)
                    sp.wait_ge(s_load, 16)

                @block.vector
                def _(dve):
                    nc.vector.tensor_copy(iota_row[:, :], iota_row0[:, :])
                    nc.vector.tensor_copy(iota_col[:, :], iota_col0[:, :])
                    if clear_weights:
                        nc.vector.memset(ew2[:, :, 0:1], 0.0)
                    if clear_rows:
                        nc.vector.memset(acc[0:clear_rows, 0:NPAD], 0.0)
            end_stage()

        def next_windows(dve, link):
            link(nc.vector.tensor_scalar(iota_row[:, :], iota_row[:, :], float(WIN), None, ALU.add))
            link(nc.vector.tensor_scalar(iota_col[:, :], iota_col[:, :], float(WIN), None, ALU.add))
            link(nc.vector.tensor_scalar(base_sb[:, :], base_sb[:, :], WIN, None, ALU.add))

        def load_indices(sp, it, h, free):
            sp.wait_ge(free, done(it * U + 2 * h + 1 - U))
            sp.dma_start(idx[:, h, :, :],
                         src_pad[ds((it * U + 2 * h) * GE, 2 * GE)].rearrange("(g p j) -> p g j", p=P, j=SUB)
                         ).then_inc(s_idx[h], 16)

        def gather_rows(pool, table, width, free):
            with pool.Fori(0, STEPS) as it:
                for u in range(U):
                    if u % 2 == 0:
                        pool.wait_ge(s_idx[u // 2], 16 * (it + 1))
                        pool.nop(nofuse=True)
                    pool.wait_ge(free, done(it * U + u - U))
                    pool.nop(nofuse=True)
                    for j in range(SUB):
                        pool.indirect_dma_start(
                            out=rows_gat[:, u, j, 0:width], out_offset=None, in_=table,
                            in_offset=bass.IndirectOffsetOnAxis(ap=idx[:, u // 2, u % 2, j:j + 1], axis=0)
                        ).then_inc(s_gat[u][j], 16)

        def edge_round(update):
            width = PR if update else ED
            gtab, wtab = (tab_pr, tab_qs) if update else (tab_p, tab_q)
            used = s_u if update else s_t
            with nc.Block() as block:
                @block.sync
                def _(sp):
                    with sp.Fori(0, STEPS) as it:
                        for u in range(U):
                            if u % 2 == 0:
                                load_indices(sp, it, u // 2, used)
                            i = it * U + u
                            first = sp.value_load(base_sb[0:1, ds(i, 1)], min_val=0, max_val=NALL - WIN)
                            sp.wait_ge(used, done(i - U))
                            sp.dma_start(rel_row[:, u, :],
                                         rel_d[ds(i * GE, GE)].rearrange("(o e) -> o e", o=1)
                                         .broadcast_to([WIN, GE])).then_inc(s_win[u], 16)
                            sp.dma_start(win[:, u, 0:width], wtab[ds(first, WIN), :]).then_inc(s_win[u], 16)

                @block.gpsimd
                def _(pool):
                    gather_rows(pool, gtab, width, used)

                @block.vector
                def _(dve):
                    def hot_of(it, u):
                        i = it * U + u
                        dve.wait_ge(s_win[u], 32 * (it + 1))
                        dve.wait_ge(used, done(i - 2))
                        nc.vector.tensor_scalar(
                            hotT[:, u % 2, :].rearrange("w (j p) -> w j p", p=P),
                            rel_row[:, u, :].rearrange("w (p j) -> w j p", j=SUB),
                            iota_col[0:WIN, 0:1], None, ALU.is_equal).then_inc(s_hotT, 1)

                    def take_z(it, u):
                        i = it * U + u
                        dve.wait_ge(s_z, done(i))
                        z = pz[u % 2][:, 0:SUB * (ED + 1)].rearrange("p (j f) -> p j f", f=ED + 1)
                        if update:
                            for j in range(SUB):
                                nc.vector.bn_stats(stats[:, ds(i * SUB + j, 1), :], z[:, j, 0:ED])
                            nc.vector.tensor_copy(rawz[:, ds(i * SUB, SUB)], z[:, :, ED]).then_inc(s_zcp, 1)
                        else:
                            nc.vector.tensor_copy(rawz[:, ds(i * SUB, SUB)], pz[u % 2][:, 0:SUB]).then_inc(s_zcp, 1)

                    dve.sem_inc(s_hotT, CREDIT)
                    dve.sem_inc(s_zcp, CREDIT)

                    def step(it, last):
                        for u in range(U):
                            if not (last and u == U - 1):
                                hot_of(it + (u + 1) // U, (u + 1) % U)
                            take_z(it, u)
                    hot_of(0, 0)
                    with dve.Fori(0, STEPS - 1) as it:
                        step(it, False)
                    step(STEPS - 1, True)

                @block.tensor
                def _(pe):
                    pe.sem_inc(s_t, CREDIT)
                    pe.sem_inc(s_u, CREDIT)
                    pe.sem_inc(s_z, CREDIT)

                    def t_of(it, u):
                        i = it * U + u
                        pe.wait_ge(s_relu, done(i - 2))
                        for j in range(SUB):
                            pe.wait_ge(s_gat[u][j], 16 * (it + 1))
                            nc.tensor.matmul(pt[u % 2][0:ED, j * P:(j + 1) * P], rows_gat[:, u, j, 0:ED],
                                             ident[:, :], start=(j == 0), stop=False, skip_group_check=True)
                        pe.wait_ge(s_hotT, done(i))
                        pe.nop(nofuse=True)
                        nc.tensor.matmul(pt[u % 2][0:ED, :], win[:, u, 0:ED], hotT[:, u % 2, :],
                                         start=False, stop=True, skip_group_check=True).then_inc(s_t, 1)
                        if update:
                            pe.wait_ge(s_urelu, done(i - 2))
                            for j in range(SUB):
                                nc.tensor.matmul(pu[u % 2][:, j * P:(j + 1) * P], rows_gat[:, u, j, ED:PR],
                                                 ident[:, :], start=(j == 0), stop=False, skip_group_check=True)
                            nc.tensor.matmul(pu[u % 2][:, :], win[:, u, ED:PR], hotT[:, u % 2, :],
                                             start=False, stop=False, skip_group_check=True)
                            pe.wait_ge(s_relu, done(i))
                            nc.tensor.matmul(pu[u % 2][:, :], wtu[:, :], tT[:, u % 2, :],
                                             start=False, stop=True, skip_group_check=True).then_inc(s_u, 1)

                    def z_of(it, u):
                        i = it * U + u
                        pe.wait_ge(s_urelu if update else s_relu, done(i))
                        pe.wait_ge(s_zcp, done(i - 2))
                        for j in range(SUB):
                            if update:
                                o = pz[u % 2][:, j * (ED + 1):(j + 1) * (ED + 1)]
                                nc.tensor.matmul(o, tT[:, u % 2, j * P:(j + 1) * P], wz[:, :], start=True, stop=False)
                                last = nc.tensor.matmul(o, uT[:, u % 2, j * P:(j + 1) * P], wv[:, :],
                                                        start=False, stop=True)
                            else:
                                last = nc.tensor.matmul(pz[u % 2][:, j:j + 1], tT[:, u % 2, j * P:(j + 1) * P],
                                                        wl[:, :], start=True, stop=True)
                        last.then_inc(s_z, 1)

                    def step(it, last):
                        for u in range(U):
                            if not (last and u == U - 1):
                                t_of(it + (u + 1) // U, (u + 1) % U)
                            z_of(it, u)
                    t_of(0, 0)
                    with pe.Fori(0, STEPS - 1) as it:
                        step(it, False)
                    step(STEPS - 1, True)

                @block.scalar
                def _(act):
                    act.preload_act_table(ACT.Relu)
                    act.sem_inc(s_relu, CREDIT)
                    act.sem_inc(s_urelu, CREDIT)
                    with act.Fori(0, STEPS) as it:
                        for u in range(U):
                            i = it * U + u
                            act.wait_ge(s_t, done(i))
                            act.wait_ge(s_z, done(i - 2))
                            nc.scalar.activation(tT[0:ED, u % 2, :], pt[u % 2][0:ED, :], ACT.Relu,
                                                 bias=eib1[:, 0:1]).then_inc(s_relu, 1)
                            if update:
                                act.wait_ge(s_u, done(i))
                                nc.scalar.activation(uT[:, u % 2, :], pu[u % 2][:, :], ACT.Relu,
                                                     bias=eub1[:, 0:1]).then_inc(s_urelu, 1)
            end_stage()
            with nc.Block() as block:
                @block.vector
                def _(dve):
                    link = chain(dve, s_dve)
                    if update:
                        me, ve, mo, vo = (stats[:, :, c] for c in (1, 2, 4, 5))
                        h = 1.0 / 2
                        link(nc.vector.tensor_tensor(tmpa[:, :], me, mo, ALU.subtract))
                        link(nc.vector.scalar_tensor_tensor(tmpa[:, :], tmpa[:, :], h * h, tmpa[:, :],
                                                            ALU.mult, ALU.mult))
                        link(nc.vector.tensor_tensor(tmpb[:, :], ve, vo, ALU.add))
                        link(nc.vector.scalar_tensor_tensor(tmpa[:, :], tmpb[:, :], 1.0 / ED, tmpa[:, :],
                                                            ALU.mult, ALU.add))
                        link(nc.vector.tensor_tensor(tmpb[:, :], me, mo, ALU.add))
                        link(nc.vector.tensor_scalar(tmpb[:, :], tmpb[:, :], h, sgw[:, 0:1], ALU.mult, ALU.mult))
                        link(nc.vector.tensor_tensor(rawz[:, :], rawz[:, :], tmpb[:, :], ALU.subtract))
                        dve.wait_ge(s_act, 1)
                        link(nc.vector.reciprocal(tmpb[:, :], tmpa[:, :]))
                        link(nc.vector.tensor_tensor(rawz[:, :], rawz[:, :], tmpb[:, :], ALU.mult))
                    link(nc.vector.tensor_scalar(tmpb[:, :], rel[:, :], iota_row[:, 0:1], None, ALU.is_ge))
                    link(nc.vector.scalar_tensor_tensor(tmpb[:, :], rel[:, :], iota_row[:, WIN - 1:WIN], tmpb[:, :],
                                                        ALU.is_le, ALU.mult))
                    dve.wait_ge(s_act, 2 if update else 1)
                    link(nc.vector.tensor_tensor(tmpb[:, :], tmpb[:, :], tmpa[:, :], ALU.mult))
                    link(nc.vector.tensor_tensor(ew2[:, :, 0], ew2[:, :, 0], tmpb[:, :], ALU.add))
                    next_windows(dve, link)

                @block.scalar
                def _(act):
                    if update:
                        act.wait_ge(s_dve, 4)
                        nc.scalar.activation(tmpa[:, :], tmpa[:, :], ACT.Sqrt, bias=eps_ln[:, 0:1]).then_inc(s_act, 1)
                        act.wait_ge(s_dve, 9)
                        nc.scalar.activation(tmpa[:, :], rawz[:, :], ACT.Sigmoid, bias=zb[:, 0:1]).then_inc(s_act, 1)
                    else:
                        nc.scalar.activation(tmpa[:, :], rawz[:, :], ACT.Sigmoid, bias=ewb[:, 0:1]).then_inc(s_act, 1)
            end_stage()

        def sum_round(kind):
            M = 2 if kind == "degree" else P
            with nc.Block() as block:
                if kind != "degree":
                    @block.sync
                    def _(sp):
                        with sp.Fori(0, STEPS) as it:
                            for h in range(2):
                                load_indices(sp, it, h, s_sum)

                    @block.gpsimd
                    def _(pool):
                        gather_rows(pool, tab_h, D, s_sum)

                @block.vector
                def _(dve):
                    dve.sem_inc(s_hot, CREDIT)
                    dve.sem_inc(s_acc, CREDIT)

                    def hot_of(it, u):
                        i = it * U + u
                        dve.wait_ge(s_sum, done(i - 2))
                        if kind == "degree":
                            nc.vector.tensor_copy(wts[:, u % 2, :, :], ew2[:, ds(i * SUB, SUB), :])
                        for j in range(SUB):
                            k = i * SUB + j
                            if kind == "weighted":
                                last = nc.vector.tensor_scalar(hot[:, u % 2, j, :], iota_row[:, :], rel[:, ds(k, 1)],
                                                               ew2[:, ds(k, 1), 0], ALU.is_equal, ALU.mult)
                            else:
                                last = nc.vector.tensor_scalar(hot[:, u % 2, j, :], iota_row[:, :], rel[:, ds(k, 1)],
                                                               None, ALU.is_equal)
                        last.then_inc(s_hot, 1)

                    def add(it, u):
                        i = it * U + u
                        first = dve.value_load(base_sb[0:1, ds(i, 1)], min_val=0, max_val=NALL - WIN)
                        a = acc[0:M, ds(first, WIN)]
                        dve.wait_ge(s_sum, done(i))
                        dve.wait_ge(s_acc, done(i - 1))
                        nc.vector.tensor_tensor(a, a, pt[u % 2][0:M, 0:WIN], ALU.add).then_inc(s_acc, 1)

                    def step(it, last):
                        for u in range(U):
                            if not (last and u == U - 1):
                                hot_of(it + (u + 1) // U, (u + 1) % U)
                            add(it, u)
                    hot_of(0, 0)
                    with dve.Fori(0, STEPS - 1) as it:
                        step(it, False)
                    step(STEPS - 1, True)

                @block.tensor
                def _(pe):
                    pe.sem_inc(s_sum, CREDIT)
                    with pe.Fori(0, STEPS) as it:
                        for u in range(U):
                            i = it * U + u
                            pe.wait_ge(s_hot, done(i))
                            pe.wait_ge(s_acc, done(i - 2))
                            for j in range(SUB):
                                if kind != "degree":
                                    pe.wait_ge(s_gat[u][j], 16 * (it + 1))
                                lhsT = wts[:, u % 2, j, :] if kind == "degree" else rows_gat[:, u, j, 0:D]
                                last = nc.tensor.matmul(pt[u % 2][0:M, 0:WIN], lhsT, hot[:, u % 2, j, :],
                                                        start=(j == 0), stop=(j == SUB - 1))
                            last.then_inc(s_sum, 1)
            end_stage()
            with nc.Block() as block:
                @block.vector
                def _(dve):
                    next_windows(dve, chain(dve, s_dve))
            end_stage()

        def bc_t(v):
            return v[:, :].unsqueeze(2).broadcast_to([P, NT, D])

        def bc_f(k):
            return rowv[:, k, :].unsqueeze(1).broadcast_to([P, NT, D])

        def layernorm_steps(dve, act_name, link, v, scratch):
            link(nc.vector.tensor_reduce(s1[:, :], v, axis=AXX, op=ALU.add))
            link(nc.vector.tensor_scalar(s1[:, :], s1[:, :], 1.0 / D, None, ALU.mult))
            link(nc.vector.tensor_tensor(v, v, bc_t(s1), ALU.subtract))
            link(nc.vector.tensor_tensor(scratch, v, v, ALU.mult))
            link(nc.vector.tensor_reduce(s2[:, :], scratch, axis=AXX, op=ALU.add))

        def layernorm(v, scratch, gain=None, shift=None, relu_to=None, before=None, add_to=None):
            with nc.Block() as block:
                @block.vector
                def _(dve):
                    link = chain(dve, s_dve)
                    for op in before or ():
                        link(op())
                    layernorm_steps(dve, None, link, v, scratch)
                    dve.wait_ge(s_act, 1)
                    link(nc.vector.reciprocal(s1[:, :], s2[:, :]))
                    link(nc.vector.tensor_tensor(v, v, bc_t(s1), ALU.mult))
                    if gain is not None:
                        link(nc.vector.tensor_tensor(v, v, bc_f(gain), ALU.mult))
                        link(nc.vector.tensor_tensor(v, v, bc_f(shift), ALU.add))
                    if add_to is not None:
                        link(nc.vector.tensor_tensor(add_to, add_to, v, ALU.add))
                    if relu_to is not None:
                        link(nc.vector.tensor_scalar(relu_to, v, 0.0, None, ALU.max))

                @block.scalar
                def _(act):
                    act.wait_ge(s_dve, len(before or ()) + 5)
                    nc.scalar.activation(s2[:, :], s2[:, :], ACT.Sqrt, bias=eps_ln[:, 0:1],
                                         scale=1.0 / D).then_inc(s_act, 1)
            end_stage()

        def transpose_project(source, weight=None, width=D, into=None, add=False, to_acc=False):
            with nc.Block() as block:
                @block.tensor
                def _(pe):
                    pe.sem_inc(s_pe, CREDIT)

                    def one(t, par):
                        pe.wait_ge(s_stage, done(t))
                        pe.wait_ge(s_dve, done(t - 2))
                        nc.tensor.transpose(pt[par][:, 0:P], stage[:, par, :], ident[:, :]).then_inc(s_pe, 1)
                        if not to_acc:
                            pe.wait_ge(s_dve, done(t))
                            pe.wait_ge(s_act, done(t - 2))
                            nc.tensor.matmul(pu[par][:, 0:width], hT[:, par, :], weight, start=True,
                                             stop=True).then_inc(s_u, 1)
                    with pe.Fori(0, NT // 2) as q:
                        one(2 * q, 0)
                        one(2 * q + 1, 1)
                    for t in range(NT // 2 * 2, NT):
                        one(t, t % 2)

                @block.vector
                def _(dve):
                    dve.sem_inc(s_dve, CREDIT)

                    def one(t, par):
                        dve.wait_ge(s_pe, done(t))
                        if to_acc:
                            nc.vector.tensor_copy(acc[:, 0:NPAD].rearrange("f (p t) -> f t p", t=NT)[:, ds(t, 1), :],
                                                  pt[par][:, 0:P].unsqueeze(1)).then_inc(s_dve, 1)
                        else:
                            dve.wait_ge(s_u, done(t - 2))
                            nc.vector.tensor_copy(hT[:, par, :], pt[par][:, 0:P]).then_inc(s_dve, 1)
                    if not to_acc:
                        dve.sem_inc(s_u, CREDIT)
                    with dve.Fori(0, NT // 2) as q:
                        one(2 * q, 0)
                        one(2 * q + 1, 1)
                    for t in range(NT // 2 * 2, NT):
                        one(t, t % 2)

                @block.scalar
                def _(act):
                    act.sem_inc(s_act, CREDIT)
                    act.sem_inc(s_stage, CREDIT)
                    act.preload_act_table(ACT.Copy)

                    def fetch(t, par):
                        act.wait_ge(s_pe, done(t - 2))
                        act.nop(nofuse=True)
                        nc.scalar.activation(stage[:, par, :].unsqueeze(1), source[:, ds(t, 1), :],
                                             ACT.Copy).then_inc(s_stage, 1)

                    def take(t, par):
                        if not to_acc:
                            act.wait_ge(s_u, done(t))
                            act.nop(nofuse=True)
                            nc.scalar.activation(into[:, ds(t, 1), 0:width], pu[par][:, 0:width].unsqueeze(1),
                                                 ACT.Copy).then_inc(s_act, 1)
                    fetch(0, 0)
                    with act.Fori(0, NT // 2) as q:
                        fetch(2 * q + 1, 1)
                        take(2 * q, 0)
                        fetch(2 * q + 2, 0)
                        take(2 * q + 1, 1)
                    take(NT - 1, 0)
            end_stage()

        def project_acc(weight, into):
            with nc.Block() as block:
                @block.tensor
                def _(pe):
                    pe.sem_inc(s_pe, CREDIT)

                    def one(t, par):
                        pe.wait_ge(s_stage, done(t))
                        pe.wait_ge(s_act, done(t - 2))
                        nc.tensor.matmul(pt[par][:, 0:D], stage[:, par, :], weight, start=True,
                                         stop=True).then_inc(s_pe, 1)
                    with pe.Fori(0, NT // 2) as q:
                        one(2 * q, 0)
                        one(2 * q + 1, 1)
                    for t in range(NT // 2 * 2, NT):
                        one(t, t % 2)

                @block.vector
                def _(dve):
                    dve.sem_inc(s_stage, CREDIT)

                    def one(t, par):
                        dve.wait_ge(s_pe, done(t - 2))
                        nc.vector.tensor_copy(stage[:, par, :].unsqueeze(1),
                                              acc[:, 0:NPAD].rearrange("f (p t) -> f t p", t=NT)[:, ds(t, 1), :]
                                              ).then_inc(s_stage, 1)
                    with dve.Fori(0, NT // 2) as q:
                        one(2 * q, 0)
                        one(2 * q + 1, 1)
                    for t in range(NT // 2 * 2, NT):
                        one(t, t % 2)

                @block.scalar
                def _(act):
                    act.sem_inc(s_act, CREDIT)
                    act.preload_act_table(ACT.Copy)

                    def one(t, par):
                        act.wait_ge(s_pe, done(t))
                        act.nop(nofuse=True)
                        nc.scalar.activation(into[:, ds(t, 1), :], pt[par][:, 0:D].unsqueeze(1),
                                             ACT.Copy).then_inc(s_act, 1)
                    with act.Fori(0, NT // 2) as q:
                        one(2 * q, 0)
                        one(2 * q + 1, 1)
                    for t in range(NT // 2 * 2, NT):
                        one(t, t % 2)
            end_stage()

        def store_tables(*pairs):
            with nc.Block() as block:
                @block.sync
                def _(sp):
                    for d_, s_ in pairs:
                        sp.dma_start(d_.rearrange("(p t) f -> p t f", t=NT), s_).then_inc(s_store, 16)
                    sp.wait_ge(s_store, 16 * len(pairs))
            end_stage()

        def degrees():
            reset_windows(clear_rows=2)
            with nc.Fori(0, rounds):
                sum_round("degree")
            with nc.Block() as block:
                @block.sync
                def _(sp):
                    sp.dma_start(deg_d, acc[0:2, 0:NPAD]).then_inc(s_store, 16)
                    sp.wait_ge(s_store, 16)
                    for r_, d_ in ((0, dinv), (1, cinv)):
                        sp.dma_start(d_[:, :], deg_d[r_, :].rearrange("(p t) -> p t", t=NT)).then_inc(s_load, 16)
                    sp.wait_ge(s_load, 32)

                @block.vector
                def _(dve):
                    link = chain(dve, s_dve)
                    dve.wait_ge(s_load, 32)
                    link(nc.vector.tensor_scalar(cinv[:, :], cinv[:, :], 1.0, None, ALU.max))
                    link(nc.vector.reciprocal(cinv[:, :], cinv[:, :]))
                    dve.wait_ge(s_act, 1)
                    link(nc.vector.reciprocal(dinv[:, :], dinv[:, :]))
                    link(nc.vector.tensor_tensor(big, h_sb[:, :, :], bc_t(dinv), ALU.mult))

                @block.scalar
                def _(act):
                    act.wait_ge(s_load, 32)
                    nc.scalar.activation(dinv[:, :], dinv[:, :], ACT.Sqrt, bias=1.0).then_inc(s_act, 1)
            end_stage()

        def gcn(weight, bias, gain, shift):
            degrees()
            store_tables((tab_h, big))
            transpose_project(big, to_acc=True)
            reset_windows()
            with nc.Fori(0, rounds):
                sum_round("weighted")
            project_acc(weight, h_sb)
            with nc.Block() as block:
                @block.vector
                def _(dve):
                    link = chain(dve, s_dve)
                    link(nc.vector.tensor_tensor(h_sb[:, :, :], h_sb[:, :, :], bc_t(dinv), ALU.mult))
                    link(nc.vector.tensor_tensor(h_sb[:, :, :], h_sb[:, :, :], bc_f(bias), ALU.add))

                @block.scalar
                def _(act):
                    act.wait_ge(s_dve, 2)
                    nc.scalar.activation(h_sb[:, :, :], h_sb[:, :, :], ACT.Gelu).then_inc(s_act, 1)
            end_stage()

        zb = sb("zb", [P, 1])
        with nc.Block() as block:
            @block.vector
            def _(dve):
                nc.vector.tensor_tensor(zb[:, :], sgw[:, 1:2], ewb[:, :], ALU.add)
                nc.vector.tensor_copy(h_sb[:, :, :], x_sb[:, :, :])
        end_stage()
        H = h_sb[:, :, :]
        layernorm(H, big, relu_to=H)
        transpose_project(h_sb, w_pq[:, :], into=big)
        store_tables((tab_p, big[:, :, 0:ED]), (tab_q[0:NPAD, :], big[:, :, ED:2 * ED]),
                     (tab_pr[:, 0:ED], big[:, :, 0:ED]), (tab_qs[0:NPAD, 0:ED], big[:, :, ED:2 * ED]))
        reset_windows(clear_weights=True)
        with nc.Fori(0, rounds):
            edge_round(False)
        gcn(w1[:, :], 0, 2, 3)
        layernorm(H, big, gain=2, shift=3)
        transpose_project(h_sb, u1[:, :], into=big)
        store_tables((tab_pr[:, ED:PR], big))
        transpose_project(h_sb, u2[:, :], into=big)
        store_tables((tab_qs[0:NPAD, ED:PR], big))
        reset_windows(clear_weights=True)
        with nc.Fori(0, rounds):
            edge_round(True)
        gcn(w2[:, :], 1, 4, 5)
        layernorm(H, big, gain=4, shift=5, add_to=x_sb[:, :, :])
        layernorm(H, big, before=[lambda: nc.vector.tensor_copy(H, x_sb[:, :, :])], relu_to=H)

        store_tables((tab_h, H))
        reset_windows(clear_rows=P)
        with nc.Fori(0, rounds):
            sum_round("plain")
        project_acc(l1b[:, :], big)
        with nc.Block() as block:
            @block.vector
            def _(dve):
                link = chain(dve, s_dve)
                link(nc.vector.tensor_tensor(big, big, bc_t(cinv), ALU.mult))
                link(nc.vector.tensor_tensor(big, big, bc_f(6), ALU.add))
        end_stage()
        transpose_project(h_sb, l1a[:, :], into=h_sb)
        with nc.Block() as block:
            @block.vector
            def _(dve):
                link = chain(dve, s_dve)
                link(nc.vector.tensor_tensor(big, big, H, ALU.add))
                link(nc.vector.tensor_tensor(H, big, big, ALU.mult))
                link(nc.vector.tensor_reduce(s1[:, :], H, axis=AXX, op=ALU.add))
                dve.wait_ge(s_act, 1)
                link(nc.vector.tensor_scalar(s1[:, :], s1[:, :], 1e-12, None, ALU.max))
                link(nc.vector.reciprocal(s1[:, :], s1[:, :]))
                link(nc.vector.tensor_tensor(big, big, bc_t(s1), ALU.mult))
                link(nc.vector.scalar_tensor_tensor(x_sb[:, :, :], big, 0.0, x_sb[:, :, :], ALU.max, ALU.add))

            @block.scalar
            def _(act):
                act.wait_ge(s_dve, 3)
                nc.scalar.activation(s1[:, :], s1[:, :], ACT.Sqrt).then_inc(s_act, 1)

            @block.sync
            def _(sp):
                sp.wait_ge(s_dve, 7)
                sp.dma_start(out[0:FULL * NT, :].rearrange("(p t) d -> p t d", t=NT),
                             x_sb[0:FULL, :, :]).then_inc(s_store, 16)
                sp.dma_start(out[FULL * NT:N, :].rearrange("(p t) d -> p t d", p=1),
                             x_sb[FULL:FULL + 1, 0:REST, :]).then_inc(s_store, 16)
                sp.wait_ge(s_store, 32)


_INS = ["x", "src", "dst", "L0_gnn_W1", "L0_gnn_b1", "L0_gnn_W2", "L0_gnn_b2", "L0_gnn_ln1_g", "L0_gnn_ln1_b",
        "L0_gnn_ln2_g", "L0_gnn_ln2_b", "L0_gnn_ei_w1", "L0_gnn_ei_b1", "L0_gnn_ei_w2", "L0_gnn_ei_b2",
        "L0_gnn_eu_w1", "L0_gnn_eu_b1", "L0_gnn_eu_w2", "L0_gnn_eu_b2", "L0_gnn_lne_g", "L0_gnn_lne_b",
        "L0_gnn_ew_w", "L0_gnn_ew_b", "L1_gnn_W", "L1_gnn_b"]


def kernel(**inputs):
    import numpy as _np
    import concourse.bacc as _bacc
    from concourse import mybir as _mybir
    from concourse.bass_utils import run_bass_kernel_spmd as _run

    nc = _bacc.Bacc("TRN2", target_bir_lowering=False, num_devices=1)
    arrays, args = {}, []
    for name in _INS:
        a = _np.ascontiguousarray(inputs[name])
        arrays[f"in_{name}_dram"] = a
        args.append(nc.dram_tensor(f"in_{name}_dram", a.shape, _mybir.dt.from_np(a.dtype), kind="ExternalInput").ap())
    args.append(nc.dram_tensor("out_dram", inputs["x"].shape, _mybir.dt.float32, kind="ExternalOutput").ap())
    build(nc, *args)
    r = _run(nc, [arrays], core_ids=[0])
    return r.results[0]["out_dram"]
```

```python
import concourse.bass as bass
from concourse import mybir
from contextlib import ExitStack

F32 = mybir.dt.float32
I32 = mybir.dt.int32
ALU = mybir.AluOpType
ACT = mybir.ActivationFunctionType
AXX = mybir.AxisListType.X
ds = bass.ds
SP = mybir.EngineType.SP
DVE = mybir.EngineType.DVE


def build(nc, x, src, dst, W1, b1, W2, b2, ln1_g, ln1_b, ln2_g, ln2_b, ei_w1, ei_b1, ei_w2, ei_b2,
          eu_w1, eu_b1, eu_w2, eu_b2, lne_g, lne_b, ew_w, ew_b, L1_W, L1_b, out):
    P = 128
    N, D = x.shape
    E = src.shape[0]
    NT = -(-N // P)
    NPAD = NT * P
    FULL = N // NT
    REST = N - FULL * NT
    SUB = 4
    GE = SUB * P
    U = 4
    G = -(-E // (GE * U)) * U
    STEPS = G // U
    EPAD = G * GE
    GP = STEPS
    WIN = 64
    MAXR = N // WIN + 1
    NALL = -(-(N + MAXR * WIN) // P) * P
    ED = ei_w2.shape[0]
    PR = ED + D
    K = G * SUB
    CREDIT = 4
    LN_EPS = 1e-5

    def done(i):
        return i + 1 + CREDIT

    ctx = ExitStack()
    with ctx:
        sb = lambda n, s, d=F32: ctx.enter_context(nc.sbuf_tensor(n, s, d))
        sem = lambda n: ctx.enter_context(nc.semaphore(n))
        dram = lambda n, s, d=F32: nc.dram_tensor(n, s, d, kind="Internal").ap()

        src_pad = dram("src_pad", (EPAD,), I32)
        dst_pad = dram("dst_pad", (EPAD,), I32)
        rel_d = dram("rel_d", (EPAD,))
        span_d = dram("span_d", (G,), I32)
        base_d = dram("base_d", (G,), I32)
        deg_d = dram("deg_d", (2, NPAD))
        tab_p = dram("tab_p", (NPAD, ED))
        tab_q = dram("tab_q", (NALL, ED))
        tab_pr = dram("tab_pr", (NPAD, PR))
        tab_qs = dram("tab_qs", (NALL, PR))
        tab_h = dram("tab_h", (NPAD, D))

        x_sb = sb("x_sb", [P, NT, D])
        h_sb = sb("h_sb", [P, NT, D])
        area = sb("area", [P, NT * D])
        big = area[:, :].rearrange("p (t d) -> p t d", d=D)
        rows_gat = area[:, 0:U * SUB * PR].rearrange("p (u j f) -> p u j f", u=U, j=SUB)
        o1 = U * SUB * PR
        rel_row = area[P - WIN:P, o1:o1 + U * GE].rearrange("p (u e) -> p u e", u=U)
        assert o1 + U * GE <= NT * D and ED + WIN == P
        acc = sb("acc", [P, NALL])
        rel = sb("rel", [P, K])
        ew = sb("ew", [P, K])
        rawz = sb("rawz", [P, K])
        tmpb = sb("tmpb", [P, K])
        idx = sb("idx", [P, 2, 2, SUB], I32)
        win = sb("win", [P, U, PR])
        hot = sb("hot", [P, U, SUB, WIN])
        wts = sb("wts", [P, U, SUB, 2])
        st16 = sb("st16", [P, U * SUB, 6])
        zw16 = sb("zw16", [P, U * SUB])
        zl16 = sb("zl16", [P, U * SUB])
        v16 = sb("v16", [P, U * SUB])
        t16 = sb("t16", [P, U * SUB])
        stage = sb("stage", [P, 2, P])
        tT = sb("tT", [P, U, GE])
        uT = sb("uT", [P, 2, GE])
        base_sb = sb("base_sb", [1, G], I32)
        iota_row0 = sb("iota_row0", [P, WIN])
        iota_row = sb("iota_row", [P, WIN])
        iota_i = sb("iota_i", [P, WIN], I32)
        iota_c = sb("iota_c", [P, 1], I32)
        iota_col0 = sb("iota_col0", [P, 1])
        iota_col = sb("iota_col", [P, 1])
        ident = sb("ident", [P, P])
        hT = sb("hT", [P, 2, P])
        rounds_sb = sb("rounds_sb", [1, 4], I32)
        s1 = sb("s1", [P, NT])
        s2 = sb("s2", [P, NT])
        dinv = sb("dinv", [P, NT])
        cinv = sb("cinv", [P, NT])
        w_pq = sb("w_pq", [P, 2 * ED])
        w1 = sb("w1", [P, D])
        w2 = sb("w2", [P, D])
        u1 = sb("u1", [P, D])
        u2 = sb("u2", [P, D])
        u3 = sb("u3", [ED, D])
        l1a = sb("l1a", [P, D])
        l1b = sb("l1b", [P, D])
        rowv = sb("rowv", [P, 7, D])
        eib1 = sb("eib1", [ED, 1])
        eub1 = sb("eub1", [P, 1])
        wz = sb("wz", [P, ED + 1])
        wv = sb("wv", [P, ED + 1])
        wl = sb("wl", [P, 1])
        eiw = sb("eiw", [ED, ED])
        eib2 = sb("eib2", [ED, 2])
        eub2 = sb("eub2", [ED, 1])
        ewT = sb("ewT", [ED, P])
        ezT = sb("ezT", [ED, P])
        euwT = sb("euwT", [ED, P])
        lvec = sb("lvec", [ED, 4])
        ewb = sb("ewb", [P, 1])
        hsgw = sb("hsgw", [P, 1])
        sgw = sb("sgw", [P, 2])
        ones = sb("ones", [ED, P])
        prod = sb("prod", [ED, 2])
        eps_ln = sb("eps_ln", [P, 1])

        pb = lambda n: ctx.enter_context(nc.psum_tensor(n, [P, 512], F32))
        pt = [pb("pt0"), pb("pt1")]
        pu = [pb("pu0"), pb("pu1")]
        pz = [pb("pz0"), pb("pz1")]
        pd = [pb("pd0"), pb("pd1")]

        s_load = sem("loaded")
        s_store = sem("stored")
        s_pool = sem("pool_step")
        s_dve = sem("dve_step")
        s_act = sem("act_step")
        s_pe = sem("pe_step")
        s_idx = [sem(f"idx_in{h}") for h in range(2)]
        s_gat = [[sem(f"rows_in{u}_{j}") for j in range(SUB)] for u in range(U)]
        s_win = [sem(f"window_in{u}") for u in range(U)]
        s_hotT = sem("hotT_ready")
        s_hot = sem("hot_ready")
        s_t = sem("t_done")
        s_relu = sem("t_relu_done")
        s_u = sem("u_done")
        s_urelu = sem("u_relu_done")
        s_z = sem("z_done")
        s_zcp = sem("z_copied")
        s_sum = sem("sum_done")
        s_acc = sem("acc_added")
        s_stage = sem("tile_staged")
        s_sig = sem("weights_made")
        s_sqrt = sem("root_done")
        s_kept = sem("weights_kept")
        all_sems = [s_load, s_store, s_pool, s_dve, s_act, s_pe, *s_idx, *sum(s_gat, []), *s_win, s_hotT, s_hot, s_t,
                    s_relu, s_u, s_urelu, s_z, s_zcp, s_sum, s_acc, s_stage, s_sig, s_sqrt, s_kept]

        assert sorted(s.num for s in all_sems) == list(range(all_sems[0].num, all_sems[0].num + len(all_sems)))

        def end_stage():
            nc.gpsimd.dma_reset()
            nc.gpsimd.sem_clear(range(all_sems[0].num, all_sems[0].num + len(all_sems)))
            nc.all_engine_barrier()

        def chain(eng, sm):
            n = [0]

            def link(ins):
                n[0] += 1
                ins.then_inc(sm, 1)
                eng.wait_ge(sm, n[0])
            return link

        with nc.Block() as block:
            @block.sync
            def _(sp):
                def load(d_, s_):
                    sp.dma_start(d_, s_).then_inc(s_load, 16)
                sp.wait_ge(s_dve, 1)
                load(x_sb[0:FULL, :, :], x[0:FULL * NT, :].rearrange("(p t) d -> p t d", t=NT))
                load(x_sb[FULL:FULL + 1, 0:REST, :], x[FULL * NT:N, :].rearrange("(p t) d -> p t d", p=1))
                load(src_pad[0:E], src)
                load(dst_pad[0:E], dst)
                col = lambda v: v.rearrange("(p o) -> p o", o=1)
                load(w_pq[:, 0:ED], ei_w1[0:D, :])
                load(w_pq[:, ED:2 * ED], ei_w1[D:2 * D, :])
                load(w1[:, :], W1)
                load(w2[:, :], W2)
                load(u1[:, :], eu_w1[0:D, :])
                load(u2[:, :], eu_w1[D:2 * D, :])
                load(u3[:, :], eu_w1[2 * D:2 * D + ED, :])
                load(l1a[:, :], L1_W[0:D, :])
                load(l1b[:, :], L1_W[D:2 * D, :])
                for k, v in enumerate((b1, b2, ln1_g, ln1_b, ln2_g, ln2_b, L1_b)):
                    load(rowv[:, k, :], v.rearrange("(o d) -> o d", o=1).broadcast_to([P, D]))
                load(eib1[:, :], col(ei_b1))
                load(eub1[:, :], col(eu_b1))
                load(eiw[:, :], ei_w2)
                load(eib2[:, 0:1], col(ei_b2))
                load(eub2[:, :], col(eu_b2))
                load(wv[:, 0:ED], eu_w2)
                load(lvec[:, 0:1], col(lne_g))
                load(lvec[:, 1:2], col(lne_b))
                load(lvec[:, 2:3], ew_w)
                load(ewb[:, :], ew_b.rearrange("(o d) -> o d", o=1).broadcast_to([P, 1]))
                nload = 3 + 9 + 1 + 7 + 10
                sp.wait_ge(s_dve, 3)
                PADE = EPAD - E
                load(src_pad[E:EPAD].rearrange("(o e) -> o e", o=1), rel[0:1, 0:PADE].bitcast(I32))
                load(dst_pad[E:EPAD].rearrange("(o e) -> o e", o=1), rawz[0:1, 0:PADE].bitcast(I32))
                sp.wait_ge(s_dve, 4)
                PASTN = (NALL - NPAD) // P
                sp.dma_start(tab_q[NPAD:NALL, :].rearrange("(p t) d -> p (t d)", p=P),
                             acc[:, 0:PASTN * ED]).then_inc(s_store, 16)
                sp.dma_start(tab_qs[NPAD:NALL, :].rearrange("(p t) d -> p (t d)", p=P),
                             acc[:, 0:PASTN * PR]).then_inc(s_store, 16)
                sp.wait_ge(s_load, 16 * (nload + 2))
                sp.wait_ge(s_store, 32)

            @block.vector
            def _(dve):
                nc.vector.memset(x_sb[:, :, :][96:P], 0.0).then_inc(s_dve, 1)
                nc.vector.memset(rel[0:1, :].bitcast(I32), 0).then_inc(s_dve, 1)
                nc.vector.memset(rawz[0:1, :].bitcast(I32), N).then_inc(s_dve, 1)
                nc.vector.memset(acc[:, :], 0.0).then_inc(s_dve, 1)
                nc.vector.memset(wts[:, :, :, 1:2], 1.0)
                nc.vector.memset(ones[:, :], 1.0)
                nc.vector.memset(eps_ln[:, :], LN_EPS)
                dve.wait_ge(s_pool, 4)
                nc.vector.tensor_copy(iota_row0[:, :], iota_i[:, :])
                nc.vector.tensor_copy(iota_col0[:, :], iota_c[:, :])

            @block.gpsimd
            def _(pool):
                nc.gpsimd.memset(ident[:, :], 0.0).then_inc(s_pool, 1)
                nc.gpsimd.iota(iota_i[:, :], pattern=[[1, WIN]], base=0, channel_multiplier=0).then_inc(s_pool, 1)
                nc.gpsimd.iota(iota_c[:, :], pattern=[[0, 1]], base=WIN - P, channel_multiplier=1).then_inc(s_pool, 1)
                pool.wait_ge(s_pool, 3)
                nc.gpsimd.affine_select(out=ident[:, :], in_=ident[:, :], compare_op=ALU.not_equal, fill=1.0,
                                        base=0, pattern=[[-1, P]], channel_multiplier=1).then_inc(s_pool, 1)
        end_stage()

        gdst_i = area[0:GP, 0:U * GE].bitcast(I32)
        gdst = area[0:GP, U * GE:2 * U * GE]
        gmin = s1[0:GP, 0:U]
        gmax = s1[0:GP, U:2 * U]
        gint = s2[0:GP, 0:2 * U].bitcast(I32)
        with nc.Block() as block:
            @block.sync
            def _(sp):
                sp.dma_start(gdst_i, dst_pad.rearrange("(p e) -> p e", p=GP)).then_inc(s_load, 16)
                sp.wait_ge(s_dve, 6 + U)
                sp.dma_start(rel_d.rearrange("(p e) -> p e", p=GP), gdst).then_inc(s_store, 16)
                sp.dma_start(base_d.rearrange("(p u) -> p u", p=GP), gint[:, 0:U]).then_inc(s_store, 16)
                sp.dma_start(span_d.rearrange("(p u) -> p u", p=GP), gint[:, U:2 * U]).then_inc(s_store, 16)
                sp.wait_ge(s_store, 48)
                sp.dma_start(base_sb[:, :], span_d.rearrange("(o g) -> o g", o=1)).then_inc(s_load, 16)
                sp.dma_start(rel[:, :].rearrange("p (g j) -> p g j", j=SUB),
                             rel_d.rearrange("(g p j) -> p g j", p=P, j=SUB)).then_inc(s_load, 16)
                sp.wait_ge(s_load, 48)

            @block.vector
            def _(dve):
                link = chain(dve, s_dve)
                dve.wait_ge(s_load, 16)
                link(nc.vector.tensor_copy(gdst, gdst_i))
                v = gdst.rearrange("p (u e) -> p u e", u=U)
                link(nc.vector.tensor_reduce(gmin, v, axis=AXX, op=ALU.min))
                link(nc.vector.tensor_reduce(gmax, v, axis=AXX, op=ALU.max))
                for u in range(U):
                    link(nc.vector.tensor_scalar(v[:, u, :], v[:, u, :], gmin[:, u:u + 1], None, ALU.subtract))
                link(nc.vector.tensor_tensor(gmax, gmax, gmin, ALU.subtract))
                link(nc.vector.tensor_copy(gint[:, 0:U], gmin))
                link(nc.vector.tensor_copy(gint[:, U:2 * U], gmax))
                dve.wait_ge(s_load, 48)
                n0 = 6 + U
                nc.vector.tensor_reduce(rounds_sb[:, 0:1], base_sb[:, :], axis=AXX, op=ALU.max).then_inc(s_dve, 1)
                dve.wait_ge(s_dve, n0 + 1)
                nc.vector.tensor_scalar(rounds_sb[:, 1:2], rounds_sb[:, 0:1], 6, None,
                                        ALU.arith_shift_right).then_inc(s_dve, 1)
                dve.wait_ge(s_dve, n0 + 2)
                nc.vector.tensor_scalar(rounds_sb[:, 2:3], rounds_sb[:, 1:2], 1, None, ALU.add).then_inc(s_dve, 1)
                nc.vector.tensor_tensor(eib2[:, 1:2], eib2[:, 0:1], eub2[:, :], ALU.add).then_inc(s_dve, 1)
                nc.vector.tensor_tensor(lvec[:, 3:4], lvec[:, 0:1], lvec[:, 2:3], ALU.mult).then_inc(s_dve, 1)
                dve.wait_ge(s_dve, n0 + 5)
                nc.vector.tensor_copy(prod[:, 0:1], lvec[:, 3:4])
                nc.vector.tensor_scalar(ewT[:, ED:P], ones[:, 0:WIN], eib2[:, 0:1], None, ALU.mult)
                nc.vector.tensor_scalar(ezT[:, ED:P], ones[:, 0:WIN], eib2[:, 1:2], None, ALU.mult)
                nc.vector.tensor_tensor(prod[:, 1:2], lvec[:, 1:2], lvec[:, 2:3], ALU.mult)
                dve.wait_ge(s_pe, 1)
                nc.vector.tensor_copy(ewT[:, 0:ED], pt[0][0:ED, 0:ED])
                nc.vector.tensor_copy(ezT[:, 0:ED], pt[0][0:ED, 0:ED])
                nc.vector.tensor_copy(euwT[:, :], pt[0][0:ED, 256:256 + P]).then_inc(s_dve, 1)
                dve.wait_ge(s_pe, 2)
                for u in range(U):
                    nc.vector.tensor_copy(win[0:ED, u, ED:PR], pt[1][0:ED, 0:D])
                nc.vector.tensor_copy(wl[:, :], pt[1][:, 128:129])
                nc.vector.tensor_copy(wz[:, :], pt[1][:, 160:160 + ED + 1])
                nc.vector.tensor_copy(wv[:, ED:ED + 1], pt[1][:, 136:137])
                nc.vector.tensor_copy(sgw[:, :], pt[1][:, 140:142])
                nc.vector.tensor_tensor(eub1[:, :], eub1[:, :], pt[1][:, 144:145], ALU.add)

            @block.tensor
            def _(pe):
                n0 = 6 + U
                pe.wait_ge(s_dve, n0 + 3)
                nc.tensor.transpose(pt[0][0:ED, 0:ED], eiw[:, :], ident[0:ED, 0:ED])
                nc.tensor.transpose(pt[0][0:ED, 256:256 + P], wv[:, 0:ED], ident[:, :]).then_inc(s_pe, 1)
                pe.wait_ge(s_dve, n0 + 6)
                mm = lambda o, l, r_: nc.tensor.matmul(o, l, r_, start=True, stop=True)
                mm(pt[1][0:ED, 0:D], ewT[:, 0:ED], u3[:, :])
                mm(pt[1][:, 128:129], ewT[:, :], lvec[:, 2:3])
                mm(pt[1][:, 160:160 + ED], ezT[:, :], ident[0:ED, 0:ED])
                mm(pt[1][:, 160 + ED:160 + ED + 1], ezT[:, :], lvec[:, 3:4])
                mm(pt[1][:, 136:137], euwT[:, :], lvec[:, 3:4])
                mm(pt[1][:, 144:145], u3[:, :], eib2[:, 0:1])
                mm(pt[1][:, 140:142], ones[:, :], prod[:, :]).then_inc(s_pe, 1)
        end_stage()
        rounds = nc.values_load(rounds_sb[0:1, 2:3], min_val=1, max_val=MAXR)

        def reset_windows(clear_weights=False, clear_rows=0):
            with nc.Block() as block:
                @block.sync
                def _(sp):
                    sp.dma_start(base_sb[:, :], base_d.rearrange("(o g) -> o g", o=1)).then_inc(s_load, 16)
                    sp.wait_ge(s_load, 16)

                @block.vector
                def _(dve):
                    nc.vector.tensor_copy(iota_row[:, :], iota_row0[:, :])
                    nc.vector.tensor_copy(iota_col[:, :], iota_col0[:, :])
                    if clear_weights:
                        nc.vector.memset(ew[:, :], 0.0)
                    if clear_rows:
                        nc.vector.memset(acc[0:clear_rows, 0:NPAD], 0.0)
            end_stage()

        def next_windows(dve, link):
            link(nc.vector.tensor_scalar(iota_row[:, :], iota_row[:, :], float(WIN), None, ALU.add))
            link(nc.vector.tensor_scalar(iota_col[:, :], iota_col[:, :], float(WIN), None, ALU.add))
            link(nc.vector.tensor_scalar(base_sb[:, :], base_sb[:, :], WIN, None, ALU.add))

        def load_indices(sp, it, h, first):
            if not first:
                for u in (2 * h, 2 * h + 1):
                    for j in range(SUB):
                        sp.wait_ge(s_gat[u][j], 16 * it)
            sp.dma_start(idx[:, h, :, :],
                         src_pad[ds((it * U + 2 * h) * GE, 2 * GE)].rearrange("(g p j) -> p g j", p=P, j=SUB)
                         ).then_inc(s_idx[h], 16)

        def gather_rows(pool, table, width, free):
            with pool.Fori(0, STEPS) as it:
                for u in range(U):
                    if u % 2 == 0:
                        pool.wait_ge(s_idx[u // 2], 16 * (it + 1))
                        pool.nop(nofuse=True)
                    pool.wait_ge(free, done(it * U + u - U))
                    pool.nop(nofuse=True)
                    for j in range(SUB):
                        pool.indirect_dma_start(
                            out=rows_gat[:, u, j, 0:width], out_offset=None, in_=table,
                            in_offset=bass.IndirectOffsetOnAxis(ap=idx[:, u // 2, u % 2, j:j + 1], axis=0)
                        ).then_inc(s_gat[u][j], 16)

        def bases_of(eng, it):
            return nc.values_load_multi_w_load_instructions(
                base_sb[0:1, ds(it * U, U)], engines=(eng,), min_val=0, max_val=NALL - WIN)[1]

        def edge_round(update):
            width = PR if update else ED
            gtab, wtab = (tab_pr, tab_qs) if update else (tab_p, tab_q)
            used = s_u if update else s_t
            LINKS = 8
            with nc.Block() as block:
                @block.sync
                def _(sp):
                    def step(it, first):
                        firsts = bases_of(SP, it)
                        for u in range(U):
                            if u % 2 == 0:
                                load_indices(sp, it, u // 2, first)
                            i = it * U + u
                            sp.wait_ge(used, done(i - U))
                            sp.dma_start(rel_row[:, u, :],
                                         rel_d[ds(i * GE, GE)].rearrange("(o e) -> o e", o=1)
                                         .broadcast_to([WIN, GE])).then_inc(s_win[u], 16)
                            sp.dma_start(win[P - WIN:P, u, 0:width], wtab[ds(firsts[u], WIN), :]
                                         ).then_inc(s_win[u], 16)
                    step(0, True)
                    with sp.Fori(1, STEPS) as it:
                        step(it, False)

                @block.gpsimd
                def _(pool):
                    gather_rows(pool, gtab, width, used)

                @block.vector
                def _(dve):
                    def hotT_of(it, u):
                        i = it * U + u
                        dve.wait_ge(s_win[u], 32 * (it + 1))
                        dve.wait_ge(s_z, done(i - U))
                        nc.vector.tensor_scalar(
                            tT[P - WIN:P, u, :].rearrange("w (j p) -> w j p", p=P),
                            rel_row[:, u, :].rearrange("w (p j) -> w j p", j=SUB),
                            iota_col[P - WIN:P, 0:1], None, ALU.is_equal).then_inc(s_hotT, 1)

                    def take_z(it, u):
                        i = it * U + u
                        dve.wait_ge(s_z, done(i))
                        z = pz[u % 2][:, 0:SUB * (ED + 1)].rearrange("p (j f) -> p j f", f=ED + 1)
                        if update:
                            for j in range(SUB):
                                nc.vector.bn_stats(st16[:, u * SUB + j, :], z[:, j, 0:ED])
                            nc.vector.tensor_copy(zw16[:, u * SUB:(u + 1) * SUB], z[:, :, ED]).then_inc(s_zcp, 1)
                        else:
                            dve.wait_ge(s_sig, done(it - 1))
                            nc.vector.tensor_copy(zl16[:, u * SUB:(u + 1) * SUB],
                                                  pz[u % 2][:, 0:SUB]).then_inc(s_zcp, 1)

                    def link(it, k, ins):
                        ins.then_inc(s_dve, 1)
                        dve.wait_ge(s_dve, it * LINKS + k)

                    def variance(it):
                        me, ve, mo, vo = (st16[:, :, c] for c in (1, 2, 4, 5))
                        dve.wait_ge(s_zcp, done(it * U + U - 1))
                        link(it, 1, nc.vector.tensor_tensor(t16[:, :], me, mo, ALU.subtract))
                        link(it, 2, nc.vector.scalar_tensor_tensor(t16[:, :], t16[:, :], 0.25, t16[:, :],
                                                                   ALU.mult, ALU.mult))
                        link(it, 3, nc.vector.tensor_tensor(v16[:, :], ve, vo, ALU.add))
                        link(it, 4, nc.vector.scalar_tensor_tensor(v16[:, :], v16[:, :], 1.0 / ED, t16[:, :],
                                                                   ALU.mult, ALU.add))
                        link(it, 5, nc.vector.tensor_tensor(t16[:, :], me, mo, ALU.add))
                        dve.wait_ge(s_sig, done(it - 1))
                        link(it, 6, nc.vector.scalar_tensor_tensor(zl16[:, :], t16[:, :], hsgw[:, 0:1], zw16[:, :],
                                                                   ALU.mult, ALU.subtract))

                    def scale(it):
                        dve.wait_ge(s_sqrt, it + 1)
                        link(it, 7, nc.vector.reciprocal(v16[:, :], v16[:, :]))
                        link(it, 8, nc.vector.tensor_tensor(zl16[:, :], zl16[:, :], v16[:, :], ALU.mult))

                    def hots_of(it):
                        for u in range(U):
                            i = it * U + u
                            dve.wait_ge(s_sum, done(i - U))
                            for j in range(SUB):
                                last = nc.vector.tensor_scalar(hot[:, u, j, :], iota_row[:, :],
                                                               rel[:, ds(i * SUB + j, 1)], None, ALU.is_equal)
                            last.then_inc(s_hot, 1)

                    def keep_weights(it):
                        dve.wait_ge(s_sig, done(it))
                        nc.vector.tensor_copy(rawz[:, ds(it * U * SUB, U * SUB)],
                                              wts[:, :, :, 0].rearrange("p u j -> p (u j)")).then_inc(s_kept, 1)

                    def add(it, u, first):
                        i = it * U + u
                        a = acc[0:2, ds(first, WIN)]
                        dve.wait_ge(s_sum, done(i))
                        dve.wait_ge(s_acc, done(i - 1))
                        nc.vector.tensor_tensor(a, a, pd[u % 2][0:2, 0:WIN], ALU.add).then_inc(s_acc, 1)

                    def step(it, first, last):
                        if not first:
                            keep_weights(it - 1)
                            firsts = bases_of(DVE, it - 1)
                        for u in range(U):
                            if not (last and u >= U - 2):
                                hotT_of(it + (u + 2) // U, (u + 2) % U)
                            take_z(it, u)
                            if not first:
                                add(it - 1, u, firsts[u])
                        if update:
                            variance(it)
                        hots_of(it)
                        if update:
                            scale(it)

                    for s_ in (s_hotT, s_zcp, s_hot, s_kept, s_acc):
                        dve.sem_inc(s_, CREDIT)
                    hotT_of(0, 0)
                    hotT_of(0, 1)
                    step(0, True, False)
                    with dve.Fori(1, STEPS - 1) as it:
                        step(it, False, False)
                    step(STEPS - 1, False, True)
                    keep_weights(STEPS - 1)
                    firsts = bases_of(DVE, STEPS - 1)
                    for u in range(U):
                        add(STEPS - 1, u, firsts[u])

                @block.tensor
                def _(pe):
                    def t_of(it, u):
                        i = it * U + u
                        pe.wait_ge(s_relu, done(i - 2))
                        for j in range(SUB):
                            pe.wait_ge(s_gat[u][j], 16 * (it + 1))
                        pe.nop(nofuse=True)
                        for j in range(SUB):
                            nc.tensor.matmul(pt[u % 2][0:ED, j * P:(j + 1) * P], rows_gat[:, u, j, 0:ED],
                                             ident[:, :], start=(j == 0), stop=False, is_transpose=True,
                                             skip_group_check=True)
                        pe.wait_ge(s_hotT, done(i))
                        pe.nop(nofuse=True)
                        nc.tensor.matmul(pt[u % 2][0:ED, :], win[P - WIN:P, u, 0:ED], tT[P - WIN:P, u, :],
                                         start=False, stop=True, skip_group_check=True).then_inc(s_t, 1)
                        if update:
                            pe.wait_ge(s_urelu, done(i - 2))
                            for j in range(SUB):
                                nc.tensor.matmul(pu[u % 2][:, j * P:(j + 1) * P], rows_gat[:, u, j, ED:PR],
                                                 ident[:, :], start=(j == 0), stop=False, is_transpose=True,
                                                 skip_group_check=True)

                    def u_of(it, u):
                        i = it * U + u
                        pe.wait_ge(s_relu, done(i))
                        nc.tensor.matmul(pu[u % 2][:, :], win[:, u, ED:PR], tT[:, u, :],
                                         start=False, stop=True, skip_group_check=True).then_inc(s_u, 1)

                    def z_of(it, u):
                        i = it * U + u
                        pe.wait_ge(s_urelu if update else s_relu, done(i))
                        pe.wait_ge(s_zcp, done(i - 2))
                        for j in range(SUB):
                            if update:
                                o = pz[u % 2][:, j * (ED + 1):(j + 1) * (ED + 1)]
                                nc.tensor.matmul(o, tT[:, u, j * P:(j + 1) * P], wz[:, :], start=True, stop=False)
                                last = nc.tensor.matmul(o, uT[:, u % 2, j * P:(j + 1) * P], wv[:, :],
                                                        start=False, stop=True)
                            else:
                                last = nc.tensor.matmul(pz[u % 2][:, j:j + 1], tT[:, u, j * P:(j + 1) * P],
                                                        wl[:, :], start=True, stop=True)
                        last.then_inc(s_z, 1)

                    def degree_of(it, u):
                        i = it * U + u
                        pe.wait_ge(s_sig, done(it))
                        pe.wait_ge(s_hot, done(i))
                        pe.wait_ge(s_acc, done(i - 2))
                        for j in range(SUB):
                            last = nc.tensor.matmul(pd[u % 2][0:2, 0:WIN], wts[:, u, j, :], hot[:, u, j, :],
                                                    start=(j == 0), stop=(j == SUB - 1))
                        last.then_inc(s_sum, 1)

                    def step(it, first, last):
                        for u in range(U):
                            if not (last and u == U - 1):
                                t_of(it + (u + 1) // U, (u + 1) % U)
                            z_of(it, u)
                            if not first:
                                degree_of(it - 1, u)
                            if update and not (last and u == U - 1):
                                u_of(it + (u + 1) // U, (u + 1) % U)
                    for s_ in (s_t, s_u, s_z, s_sum):
                        pe.sem_inc(s_, CREDIT)
                    t_of(0, 0)
                    if update:
                        u_of(0, 0)
                    step(0, True, False)
                    with pe.Fori(1, STEPS - 1) as it:
                        step(it, False, False)
                    step(STEPS - 1, False, True)
                    for u in range(U):
                        degree_of(STEPS - 1, u)

                @block.scalar
                def _(act):
                    for s_ in (s_relu, s_urelu, s_sig):
                        act.sem_inc(s_, CREDIT)

                    def weights_of(it):
                        if update:
                            act.wait_ge(s_dve, it * LINKS + 4)
                            nc.scalar.activation(v16[:, :], v16[:, :], ACT.Sqrt, bias=eps_ln[:, 0:1]).then_inc(s_sqrt, 1)
                            act.wait_ge(s_dve, it * LINKS + 8)
                        else:
                            act.wait_ge(s_zcp, done(it * U + U - 1))
                        act.wait_ge(s_kept, done(it - 1))
                        act.wait_ge(s_sum, done(it * U - 1))
                        nc.scalar.activation(wts[:, :, :, 0], zl16[:, :].rearrange("p (u j) -> p u j", u=U),
                                             ACT.Sigmoid, bias=(zb if update else ewb)[:, 0:1],
                                             scale=-1.0 if update else 1.0).then_inc(s_sig, 1)

                    def relus(it, u):
                        i = it * U + u
                        act.wait_ge(s_t, done(i))
                        act.wait_ge(s_z, done(i - 2))
                        nc.scalar.activation(tT[0:ED, u, :], pt[u % 2][0:ED, :], ACT.Relu,
                                             bias=eib1[:, 0:1]).then_inc(s_relu, 1)
                        if update:
                            act.wait_ge(s_u, done(i))
                            nc.scalar.activation(uT[:, u % 2, :], pu[u % 2][:, :], ACT.Relu,
                                                 bias=eub1[:, 0:1]).then_inc(s_urelu, 1)

                    def step(it, first):
                        for u in range(U):
                            relus(it, u)
                            if u == 0 and not first:
                                weights_of(it - 1)
                    act.preload_act_table(ACT.Sigmoid)
                    step(0, True)
                    with act.Fori(1, STEPS) as it:
                        step(it, False)
                    weights_of(STEPS - 1)
            end_stage()
            with nc.Block() as block:
                @block.vector
                def _(dve):
                    link = chain(dve, s_dve)
                    link(nc.vector.tensor_scalar(tmpb[:, :], rel[:, :], iota_row[:, 0:1], None, ALU.is_ge))
                    link(nc.vector.scalar_tensor_tensor(tmpb[:, :], rel[:, :], iota_row[:, WIN - 1:WIN], tmpb[:, :],
                                                        ALU.is_le, ALU.mult))
                    link(nc.vector.tensor_tensor(tmpb[:, :], tmpb[:, :], rawz[:, :], ALU.mult))
                    link(nc.vector.tensor_tensor(ew[:, :], ew[:, :], tmpb[:, :], ALU.add))
                    next_windows(dve, link)
            end_stage()

        def sum_round(weighted):
            bank = [pt[0], pt[1], pu[0], pu[1]]
            with nc.Block() as block:
                @block.sync
                def _(sp):
                    for h in range(2):
                        load_indices(sp, 0, h, True)
                    with sp.Fori(1, STEPS) as it:
                        for h in range(2):
                            load_indices(sp, it, h, False)

                @block.gpsimd
                def _(pool):
                    gather_rows(pool, tab_h, D, s_sum)

                @block.vector
                def _(dve):
                    dve.sem_inc(s_hot, CREDIT)
                    dve.sem_inc(s_acc, CREDIT)

                    def hot_of(it, u):
                        i = it * U + u
                        dve.wait_ge(s_sum, done(i - U))
                        for j in range(SUB):
                            k = i * SUB + j
                            if weighted:
                                last = nc.vector.tensor_scalar(hot[:, u, j, :], iota_row[:, :], rel[:, ds(k, 1)],
                                                               ew[:, ds(k, 1)], ALU.is_equal, ALU.mult)
                            else:
                                last = nc.vector.tensor_scalar(hot[:, u, j, :], iota_row[:, :], rel[:, ds(k, 1)],
                                                               None, ALU.is_equal)
                        last.then_inc(s_hot, 1)

                    def add(it, u, first):
                        i = it * U + u
                        a = acc[:, ds(first, WIN)]
                        dve.wait_ge(s_sum, done(i))
                        dve.wait_ge(s_acc, done(i - 1))
                        nc.vector.tensor_tensor(a, a, bank[u][:, 0:WIN], ALU.add).then_inc(s_acc, 1)

                    def step(it, last):
                        firsts = bases_of(DVE, it)
                        for u in range(U):
                            if not (last and u >= U - 2):
                                hot_of(it + (u + 2) // U, (u + 2) % U)
                            add(it, u, firsts[u])
                    hot_of(0, 0)
                    hot_of(0, 1)
                    with dve.Fori(0, STEPS - 1) as it:
                        step(it, False)
                    step(STEPS - 1, True)

                @block.tensor
                def _(pe):
                    pe.sem_inc(s_sum, CREDIT)
                    with pe.Fori(0, STEPS) as it:
                        for u in range(U):
                            i = it * U + u
                            pe.wait_ge(s_hot, done(i))
                            pe.wait_ge(s_acc, done(i - U))
                            for j in range(SUB):
                                pe.wait_ge(s_gat[u][j], 16 * (it + 1))
                                last = nc.tensor.matmul(bank[u][:, 0:WIN], rows_gat[:, u, j, 0:D], hot[:, u, j, :],
                                                        start=(j == 0), stop=(j == SUB - 1))
                            last.then_inc(s_sum, 1)
            end_stage()
            with nc.Block() as block:
                @block.vector
                def _(dve):
                    next_windows(dve, chain(dve, s_dve))
            end_stage()

        def bc_t(v):
            return v[:, :].unsqueeze(2).broadcast_to([P, NT, D])

        def bc_f(k):
            return rowv[:, k, :].unsqueeze(1).broadcast_to([P, NT, D])

        def layernorm_steps(dve, act_name, link, v, scratch):
            link(nc.vector.tensor_reduce(s1[:, :], v, axis=AXX, op=ALU.add))
            link(nc.vector.tensor_scalar(s1[:, :], s1[:, :], 1.0 / D, None, ALU.mult))
            link(nc.vector.tensor_tensor(v, v, bc_t(s1), ALU.subtract))
            link(nc.vector.tensor_tensor(scratch, v, v, ALU.mult))
            link(nc.vector.tensor_reduce(s2[:, :], scratch, axis=AXX, op=ALU.add))

        def layernorm(v, scratch, gain=None, shift=None, relu_to=None, before=None, add_to=None):
            with nc.Block() as block:
                @block.vector
                def _(dve):
                    link = chain(dve, s_dve)
                    for op in before or ():
                        link(op())
                    layernorm_steps(dve, None, link, v, scratch)
                    dve.wait_ge(s_act, 1)
                    link(nc.vector.reciprocal(s1[:, :], s2[:, :]))
                    link(nc.vector.tensor_tensor(v, v, bc_t(s1), ALU.mult))
                    if gain is not None:
                        link(nc.vector.tensor_tensor(v, v, bc_f(gain), ALU.mult))
                        link(nc.vector.tensor_tensor(v, v, bc_f(shift), ALU.add))
                    if add_to is not None:
                        link(nc.vector.tensor_tensor(add_to, add_to, v, ALU.add))
                    if relu_to is not None:
                        link(nc.vector.tensor_scalar(relu_to, v, 0.0, None, ALU.max))

                @block.scalar
                def _(act):
                    act.wait_ge(s_dve, len(before or ()) + 5)
                    nc.scalar.activation(s2[:, :], s2[:, :], ACT.Sqrt, bias=eps_ln[:, 0:1],
                                         scale=1.0 / D).then_inc(s_act, 1)
            end_stage()

        def transpose_project(source, weight=None, width=D, into=None, add=False, to_acc=False):
            with nc.Block() as block:
                @block.tensor
                def _(pe):
                    pe.sem_inc(s_pe, CREDIT)

                    def one(t, par):
                        pe.wait_ge(s_stage, done(t))
                        pe.wait_ge(s_dve, done(t - 2))
                        nc.tensor.transpose(pt[par][:, 0:P], stage[:, par, :], ident[:, :]).then_inc(s_pe, 1)
                        if not to_acc:
                            pe.wait_ge(s_dve, done(t))
                            pe.wait_ge(s_act, done(t - 2))
                            nc.tensor.matmul(pu[par][:, 0:width], hT[:, par, :], weight, start=True,
                                             stop=True).then_inc(s_u, 1)
                    with pe.Fori(0, NT // 2) as q:
                        one(2 * q, 0)
                        one(2 * q + 1, 1)
                    for t in range(NT // 2 * 2, NT):
                        one(t, t % 2)

                @block.vector
                def _(dve):
                    dve.sem_inc(s_dve, CREDIT)

                    def one(t, par):
                        dve.wait_ge(s_pe, done(t))
                        if to_acc:
                            nc.vector.tensor_copy(acc[:, 0:NPAD].rearrange("f (p t) -> f t p", t=NT)[:, ds(t, 1), :],
                                                  pt[par][:, 0:P].unsqueeze(1)).then_inc(s_dve, 1)
                        else:
                            dve.wait_ge(s_u, done(t - 2))
                            nc.vector.tensor_copy(hT[:, par, :], pt[par][:, 0:P]).then_inc(s_dve, 1)
                    if not to_acc:
                        dve.sem_inc(s_u, CREDIT)
                    with dve.Fori(0, NT // 2) as q:
                        one(2 * q, 0)
                        one(2 * q + 1, 1)
                    for t in range(NT // 2 * 2, NT):
                        one(t, t % 2)

                @block.scalar
                def _(act):
                    act.sem_inc(s_act, CREDIT)
                    act.sem_inc(s_stage, CREDIT)
                    act.preload_act_table(ACT.Copy)

                    def fetch(t, par):
                        act.wait_ge(s_pe, done(t - 2))
                        act.nop(nofuse=True)
                        nc.scalar.activation(stage[:, par, :].unsqueeze(1), source[:, ds(t, 1), :],
                                             ACT.Copy).then_inc(s_stage, 1)

                    def take(t, par):
                        if not to_acc:
                            act.wait_ge(s_u, done(t))
                            act.nop(nofuse=True)
                            nc.scalar.activation(into[:, ds(t, 1), 0:width], pu[par][:, 0:width].unsqueeze(1),
                                                 ACT.Copy).then_inc(s_act, 1)
                    fetch(0, 0)
                    with act.Fori(0, NT // 2) as q:
                        fetch(2 * q + 1, 1)
                        take(2 * q, 0)
                        fetch(2 * q + 2, 0)
                        take(2 * q + 1, 1)
                    take(NT - 1, 0)
            end_stage()

        def project_acc(weight, into):
            with nc.Block() as block:
                @block.tensor
                def _(pe):
                    pe.sem_inc(s_pe, CREDIT)

                    def one(t, par):
                        pe.wait_ge(s_stage, done(t))
                        pe.wait_ge(s_act, done(t - 2))
                        nc.tensor.matmul(pt[par][:, 0:D], stage[:, par, :], weight, start=True,
                                         stop=True).then_inc(s_pe, 1)
                    with pe.Fori(0, NT // 2) as q:
                        one(2 * q, 0)
                        one(2 * q + 1, 1)
                    for t in range(NT // 2 * 2, NT):
                        one(t, t % 2)

                @block.vector
                def _(dve):
                    dve.sem_inc(s_stage, CREDIT)

                    def one(t, par):
                        dve.wait_ge(s_pe, done(t - 2))
                        nc.vector.tensor_copy(stage[:, par, :].unsqueeze(1),
                                              acc[:, 0:NPAD].rearrange("f (p t) -> f t p", t=NT)[:, ds(t, 1), :]
                                              ).then_inc(s_stage, 1)
                    with dve.Fori(0, NT // 2) as q:
                        one(2 * q, 0)
                        one(2 * q + 1, 1)
                    for t in range(NT // 2 * 2, NT):
                        one(t, t % 2)

                @block.scalar
                def _(act):
                    act.sem_inc(s_act, CREDIT)
                    act.preload_act_table(ACT.Copy)

                    def one(t, par):
                        act.wait_ge(s_pe, done(t))
                        act.nop(nofuse=True)
                        nc.scalar.activation(into[:, ds(t, 1), :], pt[par][:, 0:D].unsqueeze(1),
                                             ACT.Copy).then_inc(s_act, 1)
                    with act.Fori(0, NT // 2) as q:
                        one(2 * q, 0)
                        one(2 * q + 1, 1)
                    for t in range(NT // 2 * 2, NT):
                        one(t, t % 2)
            end_stage()

        def store_tables(*pairs):
            with nc.Block() as block:
                @block.sync
                def _(sp):
                    for d_, s_ in pairs:
                        sp.dma_start(d_.rearrange("(p t) f -> p t f", t=NT), s_).then_inc(s_store, 16)
                    sp.wait_ge(s_store, 16 * len(pairs))
            end_stage()

        def degrees():
            with nc.Block() as block:
                @block.sync
                def _(sp):
                    sp.dma_start(deg_d, acc[0:2, 0:NPAD]).then_inc(s_store, 16)
                    sp.wait_ge(s_store, 16)
                    for r_, d_ in ((0, dinv), (1, cinv)):
                        sp.dma_start(d_[:, :], deg_d[r_, :].rearrange("(p t) -> p t", t=NT)).then_inc(s_load, 16)
                    sp.wait_ge(s_load, 32)

                @block.vector
                def _(dve):
                    link = chain(dve, s_dve)
                    dve.wait_ge(s_load, 32)
                    link(nc.vector.tensor_scalar(cinv[:, :], cinv[:, :], 1.0, None, ALU.max))
                    link(nc.vector.reciprocal(cinv[:, :], cinv[:, :]))
                    dve.wait_ge(s_act, 1)
                    link(nc.vector.reciprocal(dinv[:, :], dinv[:, :]))
                    link(nc.vector.tensor_tensor(big, h_sb[:, :, :], bc_t(dinv), ALU.mult))

                @block.scalar
                def _(act):
                    act.wait_ge(s_load, 32)
                    nc.scalar.activation(dinv[:, :], dinv[:, :], ACT.Sqrt, bias=1.0).then_inc(s_act, 1)
            end_stage()

        def gcn(weight, bias, gain, shift):
            degrees()
            store_tables((tab_h, big))
            transpose_project(big, to_acc=True)
            reset_windows()
            with nc.Fori(0, rounds):
                sum_round(True)
            project_acc(weight, h_sb)
            with nc.Block() as block:
                @block.vector
                def _(dve):
                    link = chain(dve, s_dve)
                    link(nc.vector.tensor_tensor(h_sb[:, :, :], h_sb[:, :, :], bc_t(dinv), ALU.mult))
                    link(nc.vector.tensor_tensor(h_sb[:, :, :], h_sb[:, :, :], bc_f(bias), ALU.add))

                @block.scalar
                def _(act):
                    act.wait_ge(s_dve, 2)
                    nc.scalar.activation(h_sb[:, :, :], h_sb[:, :, :], ACT.Gelu).then_inc(s_act, 1)
            end_stage()

        zb = sb("zb", [P, 1])
        with nc.Block() as block:
            @block.vector
            def _(dve):
                nc.vector.tensor_scalar(hsgw[:, :], sgw[:, 0:1], 0.5, None, ALU.mult)
                nc.vector.tensor_tensor(zb[:, :], sgw[:, 1:2], ewb[:, :], ALU.add)
                nc.vector.tensor_copy(h_sb[:, :, :], x_sb[:, :, :])
        end_stage()
        H = h_sb[:, :, :]
        layernorm(H, big, relu_to=H)
        transpose_project(h_sb, w_pq[:, :], into=big)
        store_tables((tab_p, big[:, :, 0:ED]), (tab_q[0:NPAD, :], big[:, :, ED:2 * ED]),
                     (tab_pr[:, 0:ED], big[:, :, 0:ED]), (tab_qs[0:NPAD, 0:ED], big[:, :, ED:2 * ED]))
        reset_windows(clear_weights=True, clear_rows=2)
        with nc.Fori(0, rounds):
            edge_round(False)
        gcn(w1[:, :], 0, 2, 3)
        layernorm(H, big, gain=2, shift=3)
        transpose_project(h_sb, u1[:, :], into=big)
        store_tables((tab_pr[:, ED:PR], big))
        transpose_project(h_sb, u2[:, :], into=big)
        store_tables((tab_qs[0:NPAD, ED:PR], big))
        reset_windows(clear_weights=True, clear_rows=2)
        with nc.Fori(0, rounds):
            edge_round(True)
        gcn(w2[:, :], 1, 4, 5)
        layernorm(H, big, gain=4, shift=5, add_to=x_sb[:, :, :])
        layernorm(H, big, before=[lambda: nc.vector.tensor_copy(H, x_sb[:, :, :])], relu_to=H)

        store_tables((tab_h, H))
        reset_windows(clear_rows=P)
        with nc.Fori(0, rounds):
            sum_round(False)
        project_acc(l1b[:, :], big)
        with nc.Block() as block:
            @block.vector
            def _(dve):
                link = chain(dve, s_dve)
                link(nc.vector.tensor_tensor(big, big, bc_t(cinv), ALU.mult))
                link(nc.vector.tensor_tensor(big, big, bc_f(6), ALU.add))
        end_stage()
        transpose_project(h_sb, l1a[:, :], into=h_sb)
        with nc.Block() as block:
            @block.vector
            def _(dve):
                link = chain(dve, s_dve)
                link(nc.vector.tensor_tensor(big, big, H, ALU.add))
                link(nc.vector.tensor_tensor(H, big, big, ALU.mult))
                link(nc.vector.tensor_reduce(s1[:, :], H, axis=AXX, op=ALU.add))
                dve.wait_ge(s_act, 1)
                link(nc.vector.tensor_scalar(s1[:, :], s1[:, :], 1e-12, None, ALU.max))
                link(nc.vector.reciprocal(s1[:, :], s1[:, :]))
                link(nc.vector.tensor_tensor(big, big, bc_t(s1), ALU.mult))
                link(nc.vector.scalar_tensor_tensor(x_sb[:, :, :], big, 0.0, x_sb[:, :, :], ALU.max, ALU.add))

            @block.scalar
            def _(act):
                act.wait_ge(s_dve, 3)
                nc.scalar.activation(s1[:, :], s1[:, :], ACT.Sqrt).then_inc(s_act, 1)

            @block.sync
            def _(sp):
                sp.wait_ge(s_dve, 7)
                sp.dma_start(out[0:FULL * NT, :].rearrange("(p t) d -> p t d", t=NT),
                             x_sb[0:FULL, :, :]).then_inc(s_store, 16)
                sp.dma_start(out[FULL * NT:N, :].rearrange("(p t) d -> p t d", p=1),
                             x_sb[FULL:FULL + 1, 0:REST, :]).then_inc(s_store, 16)
                sp.wait_ge(s_store, 32)


_INS = ["x", "src", "dst", "L0_gnn_W1", "L0_gnn_b1", "L0_gnn_W2", "L0_gnn_b2", "L0_gnn_ln1_g", "L0_gnn_ln1_b",
        "L0_gnn_ln2_g", "L0_gnn_ln2_b", "L0_gnn_ei_w1", "L0_gnn_ei_b1", "L0_gnn_ei_w2", "L0_gnn_ei_b2",
        "L0_gnn_eu_w1", "L0_gnn_eu_b1", "L0_gnn_eu_w2", "L0_gnn_eu_b2", "L0_gnn_lne_g", "L0_gnn_lne_b",
        "L0_gnn_ew_w", "L0_gnn_ew_b", "L1_gnn_W", "L1_gnn_b"]


def kernel(**inputs):
    import numpy as _np
    import concourse.bacc as _bacc
    from concourse import mybir as _mybir
    from concourse.bass_utils import run_bass_kernel_spmd as _run

    nc = _bacc.Bacc("TRN2", target_bir_lowering=False, num_devices=1)
    arrays, args = {}, []
    for name in _INS:
        a = _np.ascontiguousarray(inputs[name])
        arrays[f"in_{name}_dram"] = a
        args.append(nc.dram_tensor(f"in_{name}_dram", a.shape, _mybir.dt.from_np(a.dtype), kind="ExternalInput").ap())
    args.append(nc.dram_tensor("out_dram", inputs["x"].shape, _mybir.dt.float32, kind="ExternalOutput").ap())
    build(nc, *args)
    r = _run(nc, [arrays], core_ids=[0])
    return r.results[0]["out_dram"]
```

```python
import concourse.bass as bass
from concourse import mybir
from contextlib import ExitStack

F32 = mybir.dt.float32
I32 = mybir.dt.int32
BF16 = mybir.dt.bfloat16
ALU = mybir.AluOpType
ACT = mybir.ActivationFunctionType
AXX = mybir.AxisListType.X
ds = bass.ds
SP = mybir.EngineType.SP
DVE = mybir.EngineType.DVE


def build(nc, x, src, dst, W1, b1, W2, b2, ln1_g, ln1_b, ln2_g, ln2_b, ei_w1, ei_b1, ei_w2, ei_b2,
          eu_w1, eu_b1, eu_w2, eu_b2, lne_g, lne_b, ew_w, ew_b, L1_W, L1_b, out):
    P = 128
    N, D = x.shape
    E = src.shape[0]
    NT = -(-N // P)
    NPAD = NT * P
    FULL = N // NT
    REST = N - FULL * NT
    SUB = 4
    GE = SUB * P
    U = 4
    G = -(-E // (GE * U)) * U
    STEPS = G // U
    EPAD = G * GE
    GP = STEPS
    WIN = 64
    MAXR = N // WIN + 1
    NALL = -(-(N + MAXR * WIN) // P) * P
    ED = ei_w2.shape[0]
    PR = ED + D
    K = G * SUB
    CREDIT = 4
    LN_EPS = 1e-5

    def done(i):
        return i + 1 + CREDIT

    ctx = ExitStack()
    with ctx:
        sb = lambda n, s, d=F32: ctx.enter_context(nc.sbuf_tensor(n, s, d))
        sem = lambda n: ctx.enter_context(nc.semaphore(n))
        dram = lambda n, s, d=F32: nc.dram_tensor(n, s, d, kind="Internal").ap()

        src_pad = dram("src_pad", (EPAD,), I32)
        dst_pad = dram("dst_pad", (EPAD,), I32)
        rel_d = dram("rel_d", (EPAD,))
        span_d = dram("span_d", (G,), I32)
        base_d = dram("base_d", (G,), I32)
        deg_d = dram("deg_d", (2, NPAD))
        srcp_d = dram("srcp_d", (EPAD,), BF16)
        srct_d = dram("srct_d", (EPAD,))
        kept_d = dram("kept_d", (G, P, SUB * D))
        tab_p = dram("tab_p", (NPAD, ED + D))
        tab_q = dram("tab_q", (NALL, ED))
        tab_pr = dram("tab_pr", (NPAD, PR + D))
        tab_qs = dram("tab_qs", (NALL, PR))
        tab_h = dram("tab_h", (NPAD, D))

        x_sb = sb("x_sb", [P, NT, D])
        h_sb = sb("h_sb", [P, NT, D])
        area = sb("area", [P, NT * D])
        big = area[:, :].rearrange("p (t d) -> p t d", d=D)
        rows_gat = area[:, 0:U * SUB * (PR + D)].rearrange("p (u j f) -> p u j f", u=U, j=SUB)
        assert U * SUB * (PR + D) <= NT * D and ED + WIN == P
        rows_kept = area[:, 0:U * SUB * D].rearrange("p (u e) -> p u e", u=U)
        o1 = U * SUB * D
        hotp = area[:, o1:o1 + GE].bitcast(BF16).rearrange("p (s e) -> p s e", s=2)
        o2 = o1 + GE
        srcp_row = area[:, o2:o2 + U * GE // 2].bitcast(BF16).rearrange("p (u e) -> p u e", u=U)
        o3 = o2 + U * GE // 2
        dist = area[:, o3:o3 + GE].rearrange("p (s e) -> p s e", s=1)
        assert o3 + GE <= NT * D
        rel_rows = sb("rel_rows", [P, U, GE])
        rel_row = rel_rows[P - WIN:P, :, :]
        srct = sb("srct", [P, K])
        iota_t = sb("iota_t", [P, NT])
        dinv3 = sb("dinv3", [P, 3, NT], BF16)
        drest = sb("drest", [P, 2, NT])
        iota_ti = sb("iota_ti", [P, NT], I32)
        neg_p = sb("neg_p", [P, 1])
        wd = sb("wd", [P, U, SUB])
        wr = sb("wr", [P, U, SUB])
        junk = sb("junk", [P, SUB, NT])
        acc = sb("acc", [P, NALL])
        rel = sb("rel", [P, K])
        ew = sb("ew", [P, K])
        rawz = sb("rawz", [P, K])
        tmpb = sb("tmpb", [P, K])
        idx = sb("idx", [P, 2, 2, SUB], I32)
        win = sb("win", [P, U, PR])
        hot = sb("hot", [P, U, SUB, WIN])
        wts = sb("wts", [P, U, SUB, 2])
        st16 = sb("st16", [P, U * SUB, 6])
        zw16 = sb("zw16", [P, U * SUB])
        zl16 = sb("zl16", [P, U * SUB])
        v16 = sb("v16", [P, U * SUB])
        t16 = sb("t16", [P, U * SUB])
        stage = sb("stage", [P, 2, P])
        tT = sb("tT", [P, U, GE])
        te = sb("te", [P, 2, SUB, ED])
        uT = sb("uT", [P, 2, GE])
        base_sb = sb("base_sb", [1, G], I32)
        iota_row0 = sb("iota_row0", [P, WIN])
        iota_row = sb("iota_row", [P, WIN])
        iota_i = sb("iota_i", [P, WIN], I32)
        iota_c = sb("iota_c", [P, 1], I32)
        iota_col0 = sb("iota_col0", [P, 1])
        iota_col = sb("iota_col", [P, 1])
        ident = sb("ident", [P, P])
        hT = sb("hT", [P, 2, P])
        rounds_sb = sb("rounds_sb", [1, 4], I32)
        s1 = sb("s1", [P, NT])
        s2 = sb("s2", [P, NT])
        dinv = sb("dinv", [P, NT])
        cinv = sb("cinv", [P, NT])
        w_pq = sb("w_pq", [P, 2 * ED])
        w1 = sb("w1", [P, D])
        w2 = sb("w2", [P, D])
        u1 = sb("u1", [P, D])
        u2 = sb("u2", [P, D])
        u3 = sb("u3", [ED, D])
        l1a = sb("l1a", [P, D])
        l1b = sb("l1b", [P, D])
        rowv = sb("rowv", [P, 7, D])
        eib1 = sb("eib1", [ED, 1])
        eub1 = sb("eub1", [P, 1])
        wz = sb("wz", [P, ED + 1])
        wv = sb("wv", [P, ED + 1])
        wl4 = sb("wl4", [P, SUB, ED])
        wwb = sb("wwb", [ED, P])
        eib1_row = sb("eib1_row", [P, ED])
        eiw = sb("eiw", [ED, ED])
        eib2 = sb("eib2", [ED, 2])
        eub2 = sb("eub2", [ED, 1])
        ewT = sb("ewT", [ED, P])
        ezT = sb("ezT", [ED, P])
        euwT = sb("euwT", [ED, P])
        lvec = sb("lvec", [ED, 4])
        ewb = sb("ewb", [P, 1])
        ewl = sb("ewl", [P, 1])
        zb = sb("zb", [P, 1])
        hsgw = sb("hsgw", [P, 1])
        sgw = sb("sgw", [P, 2])
        ones = sb("ones", [ED, P])
        prod = sb("prod", [ED, 2])
        eps_ln = sb("eps_ln", [P, 1])

        pb = lambda n: ctx.enter_context(nc.psum_tensor(n, [P, 512], F32))
        pt = [pb("pt0"), pb("pt1")]
        pu = [pb("pu0"), pb("pu1")]
        pz = [pb("pz0"), pb("pz1")]
        pd = [pb("pd0"), pb("pd1")]

        s_load = sem("loaded")
        s_store = sem("stored")
        s_pool = sem("pool_step")
        s_dve = sem("dve_step")
        s_act = sem("act_step")
        s_pe = sem("pe_step")
        s_idx = [sem(f"idx_in{h}") for h in range(2)]
        s_gat = [[sem(f"rows_in{u}_{j}") for j in range(SUB)] for u in range(U)]
        s_win = [sem(f"window_in{u}") for u in range(U)]
        s_hotT = sem("hotT_ready")
        s_hot = sem("hot_ready")
        s_t = sem("t_done")
        s_relu = sem("t_relu_done")
        s_u = sem("u_done")
        s_urelu = sem("u_relu_done")
        s_z = sem("z_done")
        s_zcp = sem("z_copied")
        s_sum = sem("sum_done")
        s_acc = sem("acc_added")
        s_stage = sem("tile_staged")
        s_keep = [sem(f"rows_kept{u}") for u in range(U)]
        s_sq = sem("distance_squared")
        s_oh = sem("source_one_hot_ready")
        s_look = sem("dinv_rows_done")
        s_pick = sem("dinv_picked")
        s_w = sem("weight_times_dinv")
        s_sig = sem("weights_made")
        s_sqrt = sem("root_done")
        s_kept = sem("weights_kept")
        all_sems = [s_load, s_store, s_pool, s_dve, s_act, s_pe, *s_idx, *sum(s_gat, []), *s_win, s_hotT, s_hot, s_t,
                    s_relu, s_u, s_urelu, s_z, s_zcp, s_sum, s_acc, s_stage, s_sig, s_sqrt, s_kept,
                    *s_keep, s_sq, s_oh, s_look, s_pick, s_w]

        assert sorted(s.num for s in all_sems) == list(range(all_sems[0].num, all_sems[0].num + len(all_sems)))

        def end_stage():
            nc.gpsimd.dma_reset()
            nc.gpsimd.sem_clear(range(all_sems[0].num, all_sems[0].num + len(all_sems)))
            nc.all_engine_barrier()

        def chain(eng, sm):
            n = [0]

            def link(ins):
                n[0] += 1
                ins.then_inc(sm, 1)
                eng.wait_ge(sm, n[0])
            return link

        with nc.Block() as block:
            @block.sync
            def _(sp):
                def load(d_, s_):
                    sp.dma_start(d_, s_).then_inc(s_load, 16)
                sp.wait_ge(s_dve, 1)
                load(x_sb[0:FULL, :, :], x[0:FULL * NT, :].rearrange("(p t) d -> p t d", t=NT))
                load(x_sb[FULL:FULL + 1, 0:REST, :], x[FULL * NT:N, :].rearrange("(p t) d -> p t d", p=1))
                load(src_pad[0:E], src)
                load(dst_pad[0:E], dst)
                col = lambda v: v.rearrange("(p o) -> p o", o=1)
                load(w_pq[:, 0:ED], ei_w1[0:D, :])
                load(w_pq[:, ED:2 * ED], ei_w1[D:2 * D, :])
                load(w1[:, :], W1)
                load(w2[:, :], W2)
                load(u1[:, :], eu_w1[0:D, :])
                load(u2[:, :], eu_w1[D:2 * D, :])
                load(u3[:, :], eu_w1[2 * D:2 * D + ED, :])
                load(l1a[:, :], L1_W[0:D, :])
                load(l1b[:, :], L1_W[D:2 * D, :])
                for k, v in enumerate((b1, b2, ln1_g, ln1_b, ln2_g, ln2_b, L1_b)):
                    load(rowv[:, k, :], v.rearrange("(o d) -> o d", o=1).broadcast_to([P, D]))
                load(eib1[:, :], col(ei_b1))
                load(eib1_row[:, :], ei_b1.rearrange("(o d) -> o d", o=1).broadcast_to([P, ED]))
                load(eub1[:, :], col(eu_b1))
                load(eiw[:, :], ei_w2)
                load(eib2[:, 0:1], col(ei_b2))
                load(eub2[:, :], col(eu_b2))
                load(wv[:, 0:ED], eu_w2)
                load(lvec[:, 0:1], col(lne_g))
                load(lvec[:, 1:2], col(lne_b))
                load(lvec[:, 2:3], ew_w)
                load(ewb[:, :], ew_b.rearrange("(o d) -> o d", o=1).broadcast_to([P, 1]))
                nload = 3 + 9 + 1 + 7 + 11
                sp.wait_ge(s_dve, 3)
                PADE = EPAD - E
                load(src_pad[E:EPAD].rearrange("(o e) -> o e", o=1), rel[0:1, 0:PADE].bitcast(I32))
                load(dst_pad[E:EPAD].rearrange("(o e) -> o e", o=1), rawz[0:1, 0:PADE].bitcast(I32))
                sp.wait_ge(s_dve, 4)
                PASTN = (NALL - NPAD) // P
                sp.dma_start(tab_q[NPAD:NALL, :].rearrange("(p t) d -> p (t d)", p=P),
                             acc[:, 0:PASTN * ED]).then_inc(s_store, 16)
                sp.dma_start(tab_qs[NPAD:NALL, :].rearrange("(p t) d -> p (t d)", p=P),
                             acc[:, 0:PASTN * PR]).then_inc(s_store, 16)
                sp.wait_ge(s_load, 16 * (nload + 2))
                sp.wait_ge(s_store, 32)

            @block.vector
            def _(dve):
                nc.vector.memset(x_sb[:, :, :][96:P], 0.0).then_inc(s_dve, 1)
                nc.vector.memset(rel[0:1, :].bitcast(I32), 0).then_inc(s_dve, 1)
                nc.vector.memset(rawz[0:1, :].bitcast(I32), N).then_inc(s_dve, 1)
                nc.vector.memset(acc[:, :], 0.0).then_inc(s_dve, 1)
                nc.vector.memset(wts[:, :, :, 1:2], 1.0)
                nc.vector.memset(ones[:, :], 1.0)
                nc.vector.memset(eps_ln[:, :], LN_EPS)
                dve.wait_ge(s_pool, 5)
                nc.vector.tensor_copy(iota_t[:, :], iota_ti[:, :])
                nc.vector.tensor_scalar(neg_p[:, :], iota_c[:, :], float(P - WIN), -1.0, ALU.add, ALU.mult)
                nc.vector.tensor_copy(iota_row0[:, :], iota_i[:, :])
                nc.vector.tensor_copy(iota_col0[:, :], iota_c[:, :])

            @block.gpsimd
            def _(pool):
                nc.gpsimd.memset(ident[:, :], 0.0).then_inc(s_pool, 1)
                nc.gpsimd.iota(iota_ti[:, :], pattern=[[1, NT]], base=0, channel_multiplier=0).then_inc(s_pool, 1)
                nc.gpsimd.iota(iota_i[:, :], pattern=[[1, WIN]], base=0, channel_multiplier=0).then_inc(s_pool, 1)
                nc.gpsimd.iota(iota_c[:, :], pattern=[[0, 1]], base=WIN - P, channel_multiplier=1).then_inc(s_pool, 1)
                pool.wait_ge(s_pool, 4)
                nc.gpsimd.affine_select(out=ident[:, :], in_=ident[:, :], compare_op=ALU.not_equal, fill=1.0,
                                        base=0, pattern=[[-1, P]], channel_multiplier=1).then_inc(s_pool, 1)
        end_stage()

        gdst_i = area[0:GP, 0:U * GE].bitcast(I32)
        gdst = area[0:GP, U * GE:2 * U * GE]
        ROUND = 1.5 * 2.0 ** 23
        gsrc = h_sb[0:GP, 16:32, :].rearrange("p t d -> p (t d)")
        gq = h_sb[0:GP, 32:48, :].rearrange("p t d -> p (t d)")
        gneg = acc[0:GP, 0:U * GE]
        gsrcp = acc[0:GP, U * GE:U * GE + U * GE // 2].bitcast(BF16)
        gmin = s1[0:GP, 0:U]
        gmax = s1[0:GP, U:2 * U]
        gint = s2[0:GP, 0:2 * U].bitcast(I32)
        with nc.Block() as block:
            @block.sync
            def _(sp):
                sp.dma_start(gdst_i, dst_pad.rearrange("(p e) -> p e", p=GP)).then_inc(s_load, 16)
                sp.wait_ge(s_dve, 6 + U)
                sp.dma_start(rel_d.rearrange("(p e) -> p e", p=GP), gdst).then_inc(s_store, 16)
                sp.dma_start(base_d.rearrange("(p u) -> p u", p=GP), gint[:, 0:U]).then_inc(s_store, 16)
                sp.dma_start(span_d.rearrange("(p u) -> p u", p=GP), gint[:, U:2 * U]).then_inc(s_store, 16)
                gsrc_i = h_sb[0:GP, 0:16, :].rearrange("p t d -> p (t d)").bitcast(I32)
                sp.dma_start(gsrc_i, src_pad.rearrange("(p e) -> p e", p=GP)).then_inc(s_act, 16)
                sp.wait_ge(s_pe, 7)
                sp.dma_start(srct_d.rearrange("(p e) -> p e", p=GP), gsrc).then_inc(s_store, 16)
                sp.dma_start(srcp_d.rearrange("(p e) -> p e", p=GP), gsrcp).then_inc(s_store, 16)
                sp.wait_ge(s_store, 80)
                sp.dma_start(srct[:, :].rearrange("p (g j) -> p g j", j=SUB),
                             srct_d.rearrange("(g p j) -> p g j", p=P, j=SUB)).then_inc(s_act, 16)
                sp.wait_ge(s_act, 32)
                sp.dma_start(base_sb[:, :], span_d.rearrange("(o g) -> o g", o=1)).then_inc(s_load, 16)
                sp.dma_start(rel[:, :].rearrange("p (g j) -> p g j", j=SUB),
                             rel_d.rearrange("(g p j) -> p g j", p=P, j=SUB)).then_inc(s_load, 16)
                sp.wait_ge(s_load, 48)

            @block.vector
            def _(dve):
                link = chain(dve, s_dve)
                dve.wait_ge(s_load, 16)
                link(nc.vector.tensor_copy(gdst, gdst_i))
                v = gdst.rearrange("p (u e) -> p u e", u=U)
                link(nc.vector.tensor_reduce(gmin, v, axis=AXX, op=ALU.min))
                link(nc.vector.tensor_reduce(gmax, v, axis=AXX, op=ALU.max))
                for u in range(U):
                    link(nc.vector.tensor_scalar(v[:, u, :], v[:, u, :], gmin[:, u:u + 1], None, ALU.subtract))
                link(nc.vector.tensor_tensor(gmax, gmax, gmin, ALU.subtract))
                link(nc.vector.tensor_copy(gint[:, 0:U], gmin))
                link(nc.vector.tensor_copy(gint[:, U:2 * U], gmax))
                gs = chain(dve, s_pe)
                dve.wait_ge(s_act, 16)
                gs(nc.vector.tensor_copy(gsrc, h_sb[0:GP, 0:16, :].rearrange("p t d -> p (t d)").bitcast(I32)))
                gs(nc.vector.tensor_scalar(gq, gsrc, 1.0 / NT, None, ALU.mult))
                gs(nc.vector.tensor_scalar(gq, gq, ROUND, ROUND, ALU.add, ALU.subtract))
                gs(nc.vector.scalar_tensor_tensor(gsrc, gq, -float(NT), gsrc, ALU.mult, ALU.add))
                gs(nc.vector.tensor_scalar(gneg, gsrc, 0.0, None, ALU.is_lt))
                gs(nc.vector.scalar_tensor_tensor(gsrc, gneg, float(NT), gsrc, ALU.mult, ALU.add))
                gs(nc.vector.tensor_tensor(gsrcp, gq, gneg, ALU.subtract))
                dve.wait_ge(s_load, 48)
                n0 = 6 + U
                nc.vector.tensor_reduce(rounds_sb[:, 0:1], base_sb[:, :], axis=AXX, op=ALU.max).then_inc(s_dve, 1)
                dve.wait_ge(s_dve, n0 + 1)
                nc.vector.tensor_scalar(rounds_sb[:, 1:2], rounds_sb[:, 0:1], 6, None,
                                        ALU.arith_shift_right).then_inc(s_dve, 1)
                dve.wait_ge(s_dve, n0 + 2)
                nc.vector.tensor_scalar(rounds_sb[:, 2:3], rounds_sb[:, 1:2], 1, None, ALU.add).then_inc(s_dve, 1)
                nc.vector.tensor_tensor(eib2[:, 1:2], eib2[:, 0:1], eub2[:, :], ALU.add).then_inc(s_dve, 1)
                nc.vector.tensor_tensor(lvec[:, 3:4], lvec[:, 0:1], lvec[:, 2:3], ALU.mult).then_inc(s_dve, 1)
                dve.wait_ge(s_dve, n0 + 5)
                nc.vector.tensor_copy(prod[:, 0:1], lvec[:, 3:4])
                nc.vector.tensor_scalar(wwb[:, :], ones[:, :], lvec[:, 2:3], None, ALU.mult)
                nc.vector.tensor_scalar(ewT[:, ED:P], ones[:, 0:WIN], eib2[:, 0:1], None, ALU.mult)
                nc.vector.tensor_scalar(ezT[:, ED:P], ones[:, 0:WIN], eib2[:, 1:2], None, ALU.mult)
                nc.vector.tensor_tensor(prod[:, 1:2], lvec[:, 1:2], lvec[:, 2:3], ALU.mult)
                dve.wait_ge(s_t, 1)
                nc.vector.tensor_copy(ewT[:, 0:ED], pt[0][0:ED, 0:ED])
                nc.vector.tensor_copy(ezT[:, 0:ED], pt[0][0:ED, 0:ED])
                nc.vector.tensor_copy(euwT[:, :], pt[0][0:ED, 256:256 + P]).then_inc(s_dve, 1)
                dve.wait_ge(s_t, 2)
                for u in range(U):
                    nc.vector.tensor_copy(win[0:ED, u, ED:PR], pt[1][0:ED, 0:D])
                for j in range(SUB):
                    nc.vector.tensor_copy(wl4[:, j, :], pt[1][:, 256:256 + ED])
                nc.vector.tensor_tensor(zb[:, :], ewb[:, :], pt[1][:, 141:142], ALU.add)
                nc.vector.tensor_tensor(ewl[:, :], ewb[:, :], pt[1][:, 128:129], ALU.add)
                nc.vector.tensor_copy(wz[:, :], pt[1][:, 160:160 + ED + 1])
                nc.vector.tensor_copy(wv[:, ED:ED + 1], pt[1][:, 136:137])
                nc.vector.tensor_copy(sgw[:, :], pt[1][:, 140:142])
                nc.vector.tensor_tensor(eub1[:, :], eub1[:, :], pt[1][:, 144:145], ALU.add)

            @block.tensor
            def _(pe):
                n0 = 6 + U
                pe.wait_ge(s_dve, n0 + 3)
                nc.tensor.transpose(pt[0][0:ED, 0:ED], eiw[:, :], ident[0:ED, 0:ED])
                nc.tensor.transpose(pt[0][0:ED, 256:256 + P], wv[:, 0:ED], ident[:, :]).then_inc(s_t, 1)
                pe.wait_ge(s_dve, n0 + 6)
                mm = lambda o, l, r_: nc.tensor.matmul(o, l, r_, start=True, stop=True)
                mm(pt[1][0:ED, 0:D], ewT[:, 0:ED], u3[:, :])
                mm(pt[1][:, 256:256 + ED], wwb[:, :], ewT[:, 0:ED])
                mm(pt[1][:, 128:129], wwb[:, :], eib2[:, 0:1])
                mm(pt[1][:, 160:160 + ED], ezT[:, :], ident[0:ED, 0:ED])
                mm(pt[1][:, 160 + ED:160 + ED + 1], ezT[:, :], lvec[:, 3:4])
                mm(pt[1][:, 136:137], euwT[:, :], lvec[:, 3:4])
                mm(pt[1][:, 144:145], u3[:, :], eib2[:, 0:1])
                mm(pt[1][:, 140:142], ones[:, :], prod[:, :]).then_inc(s_t, 1)
        end_stage()
        rounds = nc.values_load(rounds_sb[0:1, 2:3], min_val=1, max_val=MAXR)

        def reset_windows(clear_weights=False, clear_rows=0):
            with nc.Block() as block:
                @block.sync
                def _(sp):
                    sp.dma_start(base_sb[:, :], base_d.rearrange("(o g) -> o g", o=1)).then_inc(s_load, 16)
                    sp.wait_ge(s_load, 16)

                @block.vector
                def _(dve):
                    nc.vector.tensor_copy(iota_row[:, :], iota_row0[:, :])
                    nc.vector.tensor_copy(iota_col[:, :], iota_col0[:, :])
                    if clear_weights:
                        nc.vector.memset(ew[:, :], 0.0)
                    if clear_rows:
                        nc.vector.memset(acc[0:clear_rows, 0:NPAD], 0.0)
            end_stage()

        def next_windows(dve, link):
            link(nc.vector.tensor_scalar(iota_row[:, :], iota_row[:, :], float(WIN), None, ALU.add))
            link(nc.vector.tensor_scalar(iota_col[:, :], iota_col[:, :], float(WIN), None, ALU.add))
            link(nc.vector.tensor_scalar(base_sb[:, :], base_sb[:, :], WIN, None, ALU.add))

        def load_indices(sp, it, h, first, keep=None):
            if not first:
                keep_rows(sp, it - 1, h, keep)
            sp.dma_start(idx[:, h, :, :],
                         src_pad[ds((it * U + 2 * h) * GE, 2 * GE)].rearrange("(g p j) -> p g j", p=P, j=SUB)
                         ).then_inc(s_idx[h], 16)

        def keep_rows(sp, it, h, keep):
            for u in (2 * h, 2 * h + 1):
                for j in range(SUB):
                    sp.wait_ge(s_gat[u][j], 16 * (it + 1))
                if keep is not None:
                    sp.dma_start(kept_d[ds(it * U + u, 1), :, :].rearrange("o p (j d) -> (o p) j d", d=D),
                                 rows_gat[:, u, :, keep:keep + D]).then_inc(s_keep[u], 16)

        def gather_rows(pool, table, width, free, keep=False):
            def step(it, first):
                for u in range(U):
                    if u % 2 == 0:
                        pool.wait_ge(s_idx[u // 2], 16 * (it + 1))
                        pool.nop(nofuse=True)
                    pool.wait_ge(free, done(it * U + u - U))
                    pool.nop(nofuse=True)
                    if keep and not first:
                        pool.wait_ge(s_keep[u], 16 * it)
                        pool.nop(nofuse=True)
                    for j in range(SUB):
                        pool.indirect_dma_start(
                            out=rows_gat[:, u, j, 0:width], out_offset=None, in_=table,
                            in_offset=bass.IndirectOffsetOnAxis(ap=idx[:, u // 2, u % 2, j:j + 1], axis=0)
                        ).then_inc(s_gat[u][j], 16)
            step(0, True)
            with pool.Fori(1, STEPS) as it:
                step(it, False)

        def bases_of(eng, it):
            return nc.values_load_multi_w_load_instructions(
                base_sb[0:1, ds(it * U, U)], engines=(eng,), min_val=0, max_val=NALL - WIN)[1]

        def edge_round(update):
            width = PR if update else ED
            gtab, wtab = (tab_pr, tab_qs) if update else (tab_p, tab_q)
            used = s_u if update else s_t
            LINKS = 8
            with nc.Block() as block:
                @block.sync
                def _(sp):
                    def step(it, first):
                        firsts = bases_of(SP, it)
                        for u in range(U):
                            if u % 2 == 0:
                                load_indices(sp, it, u // 2, first, keep=width)
                            i = it * U + u
                            sp.wait_ge(used, done(i - U))
                            sp.dma_start(rel_row[:, u, :],
                                         rel_d[ds(i * GE, GE)].rearrange("(o e) -> o e", o=1)
                                         .broadcast_to([WIN, GE])).then_inc(s_win[u], 16)
                            sp.dma_start(win[P - WIN:P, u, 0:width], wtab[ds(firsts[u], WIN), :]
                                         ).then_inc(s_win[u], 16)
                    step(0, True)
                    with sp.Fori(1, STEPS) as it:
                        step(it, False)
                    for h in range(2):
                        keep_rows(sp, STEPS - 1, h, width)
                    for u in range(U):
                        sp.wait_ge(s_keep[u], 16 * STEPS)

                @block.gpsimd
                def _(pool):
                    gather_rows(pool, gtab, width + D, used, keep=True)

                @block.vector
                def _(dve):
                    def hotT_of(it, u):
                        i = it * U + u
                        dve.wait_ge(s_win[u], 32 * (it + 1))
                        dve.wait_ge(s_z, done(i - U))
                        nc.vector.tensor_scalar(
                            tT[P - WIN:P, u, :].rearrange("w (j p) -> w j p", p=P),
                            rel_row[:, u, :].rearrange("w (p j) -> w j p", j=SUB),
                            iota_col[P - WIN:P, 0:1], None, ALU.is_equal).then_inc(s_hotT, 1)

                    def take_z(it, u):
                        i = it * U + u
                        if update:
                            dve.wait_ge(s_z, done(i))
                            z = pz[u % 2][:, 0:SUB * (ED + 1)].rearrange("p (j f) -> p j f", f=ED + 1)
                            for j in range(SUB):
                                nc.vector.bn_stats(st16[:, u * SUB + j, :], z[:, j, 0:ED])
                            nc.vector.tensor_copy(zw16[:, u * SUB:(u + 1) * SUB], z[:, :, ED]).then_inc(s_zcp, 1)
                        else:
                            dve.wait_ge(s_z, done(i))
                            dve.wait_ge(s_zcp, done(i - 2))
                            q = pz[u % 2][:, 0:SUB * ED].rearrange("p (j f) -> p j f", f=ED)
                            nc.vector.tensor_tensor(te[:, u % 2, :, :], rows_gat[:, u, :, 0:ED], q, ALU.add
                                                    ).then_inc(s_t, 1)
                            dve.wait_ge(s_t, done(i))
                            nc.vector.scalar_tensor_tensor(te[:, u % 2, :, :].rearrange("p j f -> p (j f)"),
                                                           te[:, u % 2, :, :].rearrange("p j f -> p (j f)"), 0.0,
                                                           wl4[:, :, :].rearrange("p j f -> p (j f)"),
                                                           ALU.max, ALU.mult).then_inc(s_relu, 1)
                            dve.wait_ge(s_relu, done(i))
                            dve.wait_ge(s_sig, done(it - 1))
                            nc.vector.tensor_reduce(zl16[:, u * SUB:(u + 1) * SUB], te[:, u % 2, :, :],
                                                    axis=AXX, op=ALU.add).then_inc(s_zcp, 1)

                    def link(it, k, ins):
                        ins.then_inc(s_dve, 1)
                        dve.wait_ge(s_dve, it * LINKS + k)

                    def variance(it):
                        me, ve, mo, vo = (st16[:, :, c] for c in (1, 2, 4, 5))
                        dve.wait_ge(s_zcp, done(it * U + U - 1))
                        link(it, 1, nc.vector.tensor_tensor(t16[:, :], me, mo, ALU.subtract))
                        link(it, 2, nc.vector.scalar_tensor_tensor(t16[:, :], t16[:, :], 0.25, t16[:, :],
                                                                   ALU.mult, ALU.mult))
                        link(it, 3, nc.vector.tensor_tensor(v16[:, :], ve, vo, ALU.add))
                        link(it, 4, nc.vector.scalar_tensor_tensor(v16[:, :], v16[:, :], 1.0 / ED, t16[:, :],
                                                                   ALU.mult, ALU.add))
                        link(it, 5, nc.vector.tensor_tensor(t16[:, :], me, mo, ALU.add))
                        dve.wait_ge(s_sig, done(it - 1))
                        link(it, 6, nc.vector.scalar_tensor_tensor(zl16[:, :], t16[:, :], hsgw[:, 0:1], zw16[:, :],
                                                                   ALU.mult, ALU.subtract))

                    def scale(it):
                        dve.wait_ge(s_sqrt, it + 1)
                        link(it, 7, nc.vector.reciprocal(v16[:, :], v16[:, :]))
                        link(it, 8, nc.vector.tensor_tensor(zl16[:, :], zl16[:, :], v16[:, :], ALU.mult))

                    def hot_of(it, u):
                        i = it * U + u
                        dve.wait_ge(s_sum, done(i - U))
                        for j in range(SUB):
                            last = nc.vector.tensor_scalar(hot[:, u, j, :], iota_row[:, :],
                                                           rel[:, ds(i * SUB + j, 1)], None, ALU.is_equal)
                        last.then_inc(s_hot, 1)

                    def keep_weights(it):
                        dve.wait_ge(s_sig, done(it))
                        nc.vector.tensor_copy(rawz[:, ds(it * U * SUB, U * SUB)],
                                              wts[:, :, :, 0].rearrange("p u j -> p (u j)")).then_inc(s_kept, 1)

                    def add(it, u, first):
                        i = it * U + u
                        a = acc[0:2, ds(first, WIN)]
                        dve.wait_ge(s_sum, done(it * U + U - 1))
                        dve.wait_ge(s_acc, done(i - 1))
                        nc.vector.tensor_tensor(a, a, pd[u % 2][0:2, u // 2 * WIN:(u // 2 + 1) * WIN],
                                                ALU.add).then_inc(s_acc, 1)

                    def step(it, behind, last):
                        if behind > 1:
                            keep_weights(it - 2)
                            firsts = bases_of(DVE, it - 2)
                        for u in range(U):
                            if not (last and u >= U - 2):
                                hotT_of(it + (u + 2) // U, (u + 2) % U)
                            take_z(it, u)
                            if behind > 1:
                                add(it - 2, u, firsts[u])
                            if behind > 0:
                                hot_of(it - 1, u)
                                if update and u == 1:
                                    scale(it - 1)
                        if update:
                            variance(it)

                    for s_ in (s_hotT, s_zcp, s_hot, s_kept, s_acc) + (() if update else (s_t, s_relu)):
                        dve.sem_inc(s_, CREDIT)
                    hotT_of(0, 0)
                    hotT_of(0, 1)
                    step(0, 0, False)
                    step(1, 1, False)
                    with dve.Fori(2, STEPS - 1) as it:
                        step(it, 2, False)
                    step(STEPS - 1, 2, True)
                    if update:
                        scale(STEPS - 1)
                    for it in (STEPS - 2, STEPS - 1):
                        keep_weights(it)
                        firsts = bases_of(DVE, it)
                        for u in range(U):
                            add(it, u, firsts[u])
                            if it < STEPS - 1:
                                hot_of(it + 1, u)

                @block.tensor
                def _(pe):
                    def t_of(it, u):
                        i = it * U + u
                        pe.wait_ge(s_relu, done(i - 2))
                        for j in range(SUB):
                            pe.wait_ge(s_gat[u][j], 16 * (it + 1))
                        pe.nop(nofuse=True)
                        for j in range(SUB):
                            nc.tensor.matmul(pt[u % 2][0:ED, j * P:(j + 1) * P], rows_gat[:, u, j, 0:ED],
                                             ident[:, :], start=(j == 0), stop=False, is_transpose=True,
                                             skip_group_check=True)
                        pe.wait_ge(s_hotT, done(i))
                        pe.nop(nofuse=True)
                        nc.tensor.matmul(pt[u % 2][0:ED, :], win[P - WIN:P, u, 0:ED], tT[P - WIN:P, u, :],
                                         start=False, stop=True, skip_group_check=True).then_inc(s_t, 1)
                        if update:
                            pe.wait_ge(s_urelu, done(i - 2))
                            for j in range(SUB):
                                nc.tensor.matmul(pu[u % 2][:, j * P:(j + 1) * P], rows_gat[:, u, j, ED:PR],
                                                 ident[:, :], start=(j == 0), stop=False, is_transpose=True,
                                                 skip_group_check=True)

                    def u_of(it, u):
                        i = it * U + u
                        pe.wait_ge(s_relu, done(i))
                        nc.tensor.matmul(pu[u % 2][:, :], win[:, u, ED:PR], tT[:, u, :],
                                         start=False, stop=True, skip_group_check=True).then_inc(s_u, 1)

                    def z_of(it, u):
                        i = it * U + u
                        pe.wait_ge(s_urelu if update else s_relu, done(i))
                        pe.wait_ge(s_zcp, done(i - 2))
                        for j in range(SUB):
                            if update:
                                o = pz[u % 2][:, j * (ED + 1):(j + 1) * (ED + 1)]
                                nc.tensor.matmul(o, tT[:, u, j * P:(j + 1) * P], wz[:, :], start=True, stop=False)
                                last = nc.tensor.matmul(o, uT[:, u % 2, j * P:(j + 1) * P], wv[:, :],
                                                        start=False, stop=True)
                            else:
                                last = nc.tensor.matmul(pz[u % 2][:, j:j + 1], tT[:, u, j * P:(j + 1) * P],
                                                        wl[:, :], start=True, stop=True)
                        last.then_inc(s_z, 1)

                    def degree_of(it, u):
                        i = it * U + u
                        pe.wait_ge(s_sig, done(it))
                        pe.wait_ge(s_hot, done(i))
                        pe.wait_ge(s_acc, done(it * U - 1))
                        for j in range(SUB):
                            last = nc.tensor.matmul(pd[u % 2][0:2, u // 2 * WIN:(u // 2 + 1) * WIN],
                                                    wts[:, u, j, :], hot[:, u, j, :],
                                                    start=(j == 0), stop=(j == SUB - 1))
                        last.then_inc(s_sum, 1)

                    def q_of(it, u):
                        i = it * U + u
                        pe.wait_ge(s_hotT, done(i))
                        pe.wait_ge(s_zcp, done(i - 2))
                        for j in range(SUB):
                            pe.wait_ge(s_gat[u][j], 16 * (it + 1))
                        pe.nop(nofuse=True)
                        for j in range(SUB):
                            last = nc.tensor.matmul(pz[u % 2][:, j * ED:(j + 1) * ED], tT[P - WIN:P, u, j * P:(j + 1) * P],
                                                    win[P - WIN:P, u, 0:ED], start=True, stop=True)
                        last.then_inc(s_z, 1)

                    def step(it, first, last):
                        for u in range(U):
                            if update:
                                if not (last and u == U - 1):
                                    t_of(it + (u + 1) // U, (u + 1) % U)
                                z_of(it, u)
                                if not (last and u == U - 1):
                                    u_of(it + (u + 1) // U, (u + 1) % U)
                            else:
                                q_of(it, u)
                        if not first:
                            for u in range(U):
                                degree_of(it - 1, u)
                    for s_ in (s_z, s_sum) + ((s_t, s_u) if update else ()):
                        pe.sem_inc(s_, CREDIT)
                    if update:
                        t_of(0, 0)
                        u_of(0, 0)
                    step(0, True, False)
                    with pe.Fori(1, STEPS - 1) as it:
                        step(it, False, False)
                    step(STEPS - 1, False, True)
                    for u in range(U):
                        degree_of(STEPS - 1, u)

                @block.scalar
                def _(act):
                    for s_ in (s_sig,) + ((s_relu, s_urelu) if update else ()):
                        act.sem_inc(s_, CREDIT)

                    def root_of(it):
                        act.wait_ge(s_dve, it * LINKS + 4)
                        nc.scalar.activation(v16[:, :], v16[:, :], ACT.Sqrt, bias=eps_ln[:, 0:1]).then_inc(s_sqrt, 1)

                    def weights_of(it):
                        if update:
                            act.wait_ge(s_dve, it * LINKS + 8)
                        else:
                            act.wait_ge(s_zcp, done(it * U + U - 1))
                        act.wait_ge(s_kept, done(it - 1))
                        act.wait_ge(s_sum, done(it * U - 1))
                        nc.scalar.activation(wts[:, :, :, 0], zl16[:, :].rearrange("p (u j) -> p u j", u=U),
                                             ACT.Sigmoid, bias=(zb if update else ewl)[:, 0:1],
                                             scale=-1.0 if update else 1.0).then_inc(s_sig, 1)

                    def relus(it, u):
                        i = it * U + u
                        act.wait_ge(s_t, done(i))
                        act.wait_ge(s_z, done(i - 2))
                        nc.scalar.activation(tT[0:ED, u, :], pt[u % 2][0:ED, :], ACT.Relu,
                                             bias=eib1[:, 0:1]).then_inc(s_relu, 1)
                        act.wait_ge(s_u, done(i))
                        nc.scalar.activation(uT[:, u % 2, :], pu[u % 2][:, :], ACT.Relu,
                                             bias=eub1[:, 0:1]).then_inc(s_urelu, 1)

                    def step(it, first):
                        for u in range(U):
                            if update:
                                relus(it, u)
                            if update and u == 0 and not first:
                                root_of(it - 1)
                            if u == 2 and not first:
                                weights_of(it - 1)
                    act.preload_act_table(ACT.Sigmoid)
                    step(0, True)
                    with act.Fori(1, STEPS) as it:
                        step(it, False)
                    if update:
                        root_of(STEPS - 1)
                    weights_of(STEPS - 1)
            end_stage()
            with nc.Block() as block:
                @block.vector
                def _(dve):
                    link = chain(dve, s_dve)
                    link(nc.vector.tensor_scalar(tmpb[:, :], rel[:, :], iota_row[:, 0:1], None, ALU.is_ge))
                    link(nc.vector.scalar_tensor_tensor(tmpb[:, :], rel[:, :], iota_row[:, WIN - 1:WIN], tmpb[:, :],
                                                        ALU.is_le, ALU.mult))
                    link(nc.vector.tensor_tensor(tmpb[:, :], tmpb[:, :], rawz[:, :], ALU.mult))
                    link(nc.vector.tensor_tensor(ew[:, :], ew[:, :], tmpb[:, :], ALU.add))
                    next_windows(dve, link)
            end_stage()

        def sum_kept_round():
            bank = [pt[0], pt[1], pu[0], pu[1]]

            def look_at(u, j):
                return (pz + pd)[u][:, j * NT:(j + 1) * NT]
            with nc.Block() as block:
                @block.sync
                def _(sp):
                    def load_sources(it, u):
                        i = it * U + u
                        sp.wait_ge(s_sq, done(i - U))
                        sp.dma_start(srcp_row[:, u, :],
                                     srcp_d[ds(i * GE, GE)].rearrange("(o e) -> o e", o=1)
                                     .broadcast_to([P, GE])).then_inc(s_win[u], 16)

                    def step(it, last):
                        for u in range(U):
                            i = it * U + u
                            if not (last and u >= U - 3):
                                load_sources(it + (u + 3) // U, (u + 3) % U)
                            sp.wait_ge(s_sum, done(i - U))
                            sp.dma_start(rows_kept[:, u, :], kept_d[ds(i, 1), :, :].rearrange("o p f -> (o p) f")
                                         ).then_inc(s_gat[u][0], 16)
                    for u in range(3):
                        load_sources(0, u)
                    with sp.Fori(0, STEPS - 1) as it:
                        step(it, False)
                    step(STEPS - 1, True)

                @block.scalar
                def _(act):
                    act.preload_act_table(ACT.Relu)
                    act.sem_inc(s_sq, CREDIT)
                    act.sem_inc(s_oh, CREDIT)
                    with act.Fori(0, STEPS) as it:
                        for u in range(U):
                            i = it * U + u
                            act.wait_ge(s_win[u], 16 * (it + 1))
                            act.wait_ge(s_oh, done(i - 1))
                            nc.scalar.activation(dist[:, 0, :], srcp_row[:, u, :], ACT.Square,
                                                 bias=neg_p[:, 0:1]).then_inc(s_sq, 1)
                            act.wait_ge(s_sq, done(i))
                            act.wait_ge(s_look, done(i - 2))
                            nc.scalar.activation(hotp[:, u % 2, :], dist[:, 0, :], ACT.Relu,
                                                 bias=1.0, scale=-1.0).then_inc(s_oh, 1)

                @block.tensor
                def _(pe):
                    pe.sem_inc(s_sum, CREDIT)
                    pe.sem_inc(s_look, CREDIT)

                    def look(it, u):
                        i = it * U + u
                        pe.wait_ge(s_oh, done(i))
                        pe.wait_ge(s_pick, done(i - U))
                        v = hotp[:, u % 2, :].rearrange("n (p j) -> n j p", j=SUB)
                        for j in range(SUB):
                            for k in range(3):
                                last = nc.tensor.matmul(look_at(u, j), v[:, j, :], dinv3[:, k, :],
                                                        start=(k == 0), stop=(k == 2))
                        last.then_inc(s_look, 1)

                    def step(it, last):
                        for u in range(U):
                            i = it * U + u
                            if not (last and u >= U - 3):
                                look(it + (u + 3) // U, (u + 3) % U)
                            pe.wait_ge(s_hot, done(i))
                            pe.wait_ge(s_acc, done(i - U))
                            pe.wait_ge(s_gat[u][0], 16 * (it + 1))
                            for j in range(SUB):
                                mm = nc.tensor.matmul(bank[u][:, 0:WIN], rows_kept[:, u, j * D:(j + 1) * D],
                                                      hot[:, u, j, :], start=(j == 0), stop=(j == SUB - 1))
                            mm.then_inc(s_sum, 1)
                    for u in range(3):
                        look(0, u)
                    with pe.Fori(0, STEPS - 1) as it:
                        step(it, False)
                    step(STEPS - 1, True)

                @block.vector
                def _(dve):
                    for s_ in (s_hot, s_acc, s_pick, s_w):
                        dve.sem_inc(s_, CREDIT)

                    def pick(it, u):
                        i = it * U + u
                        dve.wait_ge(s_look, done(i))
                        dve.wait_ge(s_w, done(i - U))
                        for j in range(SUB):
                            last = nc.vector.scalar_tensor_tensor(
                                junk[:, j, :], iota_t[:, :],
                                srct[:, ds(i * SUB + j, 1)], look_at(u, j), ALU.is_equal, ALU.mult,
                                accum_out=wd[:, u, j:j + 1])
                        last.then_inc(s_pick, 1)

                    def weigh(it, u):
                        i = it * U + u
                        dve.wait_ge(s_pick, done(i))
                        nc.vector.tensor_tensor(wr[:, u, :], wd[:, u, :], ew[:, ds(i * SUB, SUB)],
                                                ALU.mult).then_inc(s_w, 1)

                    def hot_of(it, u):
                        i = it * U + u
                        dve.wait_ge(s_w, done(i))
                        dve.wait_ge(s_sum, done(i - U))
                        for j in range(SUB):
                            last = nc.vector.tensor_scalar(hot[:, u, j, :], iota_row[:, :],
                                                           rel[:, ds(i * SUB + j, 1)], wr[:, u, j:j + 1],
                                                           ALU.is_equal, ALU.mult)
                        last.then_inc(s_hot, 1)

                    def add(it, u, first):
                        i = it * U + u
                        a = acc[:, ds(first, WIN)]
                        dve.wait_ge(s_sum, done(i))
                        dve.wait_ge(s_acc, done(i - 1))
                        nc.vector.tensor_tensor(a, a, bank[u][:, 0:WIN], ALU.add).then_inc(s_acc, 1)

                    def step(it, last):
                        for u in range(U):
                            if not (last and u >= U - 2):
                                weigh(it + (u + 2) // U, (u + 2) % U)
                            if not (last and u >= U - 3):
                                pick(it + (u + 3) // U, (u + 3) % U)
                            if not (last and u >= U - 2):
                                hot_of(it + (u + 2) // U, (u + 2) % U)
                            if u == 0:
                                firsts = bases_of(DVE, it)
                            add(it, u, firsts[u])
                    pick(0, 0)
                    for u in range(2):
                        weigh(0, u)
                        pick(0, u + 1)
                        hot_of(0, u)
                    with dve.Fori(0, STEPS - 1) as it:
                        step(it, False)
                    step(STEPS - 1, True)
            end_stage()
            with nc.Block() as block:
                @block.vector
                def _(dve):
                    next_windows(dve, chain(dve, s_dve))
            end_stage()

        def sum_round():
            bank = [pt[0], pt[1], pu[0], pu[1]]
            with nc.Block() as block:
                @block.sync
                def _(sp):
                    for h in range(2):
                        load_indices(sp, 0, h, True)
                    with sp.Fori(1, STEPS) as it:
                        for h in range(2):
                            load_indices(sp, it, h, False)

                @block.gpsimd
                def _(pool):
                    gather_rows(pool, tab_h, D, s_sum)

                @block.vector
                def _(dve):
                    dve.sem_inc(s_hot, CREDIT)
                    dve.sem_inc(s_acc, CREDIT)

                    def hot_of(it, u):
                        i = it * U + u
                        dve.wait_ge(s_sum, done(i - U))
                        for j in range(SUB):
                            k = i * SUB + j
                            last = nc.vector.tensor_scalar(hot[:, u, j, :], iota_row[:, :], rel[:, ds(k, 1)],
                                                           None, ALU.is_equal)
                        last.then_inc(s_hot, 1)

                    def add(it, u, first):
                        i = it * U + u
                        a = acc[:, ds(first, WIN)]
                        dve.wait_ge(s_sum, done(i))
                        dve.wait_ge(s_acc, done(i - 1))
                        nc.vector.tensor_tensor(a, a, bank[u][:, 0:WIN], ALU.add).then_inc(s_acc, 1)

                    def step(it, last):
                        firsts = bases_of(DVE, it)
                        for u in range(U):
                            if not (last and u >= U - 2):
                                hot_of(it + (u + 2) // U, (u + 2) % U)
                            add(it, u, firsts[u])
                    hot_of(0, 0)
                    hot_of(0, 1)
                    with dve.Fori(0, STEPS - 1) as it:
                        step(it, False)
                    step(STEPS - 1, True)

                @block.tensor
                def _(pe):
                    pe.sem_inc(s_sum, CREDIT)
                    with pe.Fori(0, STEPS) as it:
                        for u in range(U):
                            i = it * U + u
                            pe.wait_ge(s_hot, done(i))
                            pe.wait_ge(s_acc, done(i - U))
                            for j in range(SUB):
                                pe.wait_ge(s_gat[u][j], 16 * (it + 1))
                                last = nc.tensor.matmul(bank[u][:, 0:WIN], rows_gat[:, u, j, 0:D], hot[:, u, j, :],
                                                        start=(j == 0), stop=(j == SUB - 1))
                            last.then_inc(s_sum, 1)
            end_stage()
            with nc.Block() as block:
                @block.vector
                def _(dve):
                    next_windows(dve, chain(dve, s_dve))
            end_stage()

        def bc_t(v):
            return v[:, :].unsqueeze(2).broadcast_to([P, NT, D])

        def bc_f(k):
            return rowv[:, k, :].unsqueeze(1).broadcast_to([P, NT, D])

        def layernorm_steps(dve, act_name, link, v, scratch):
            link(nc.vector.tensor_reduce(s1[:, :], v, axis=AXX, op=ALU.add))
            link(nc.vector.tensor_scalar(s1[:, :], s1[:, :], 1.0 / D, None, ALU.mult))
            link(nc.vector.tensor_tensor(v, v, bc_t(s1), ALU.subtract))
            link(nc.vector.tensor_tensor(scratch, v, v, ALU.mult))
            link(nc.vector.tensor_reduce(s2[:, :], scratch, axis=AXX, op=ALU.add))

        def layernorm(v, scratch, gain=None, shift=None, relu_to=None, before=None, add_to=None):
            with nc.Block() as block:
                @block.vector
                def _(dve):
                    link = chain(dve, s_dve)
                    for op in before or ():
                        link(op())
                    layernorm_steps(dve, None, link, v, scratch)
                    dve.wait_ge(s_act, 1)
                    link(nc.vector.reciprocal(s1[:, :], s2[:, :]))
                    link(nc.vector.tensor_tensor(v, v, bc_t(s1), ALU.mult))
                    if gain is not None:
                        link(nc.vector.tensor_tensor(v, v, bc_f(gain), ALU.mult))
                        link(nc.vector.tensor_tensor(v, v, bc_f(shift), ALU.add))
                    if add_to is not None:
                        link(nc.vector.tensor_tensor(add_to, add_to, v, ALU.add))
                    if relu_to is not None:
                        link(nc.vector.tensor_scalar(relu_to, v, 0.0, None, ALU.max))

                @block.scalar
                def _(act):
                    act.wait_ge(s_dve, len(before or ()) + 5)
                    nc.scalar.activation(s2[:, :], s2[:, :], ACT.Sqrt, bias=eps_ln[:, 0:1],
                                         scale=1.0 / D).then_inc(s_act, 1)
            end_stage()

        def transpose_project(source, weight=None, width=D, into=None, add=False, to_acc=False):
            TB = GE // P
            FULLS = NT // TB
            tails = [(FULLS, NT - FULLS * TB)] if NT % TB else []
            staged, turned = tT[:, 0:2, :], tT[:, 2:4, :]
            assert FULLS % 2 == 0 and FULLS > 2 and width <= P

            def slots(row, n):
                return row[:, 0:n * P].rearrange("p (t f) -> p t f", f=P)

            with nc.Block() as block:
                @block.tensor
                def _(pe):
                    pe.sem_inc(s_pe, CREDIT)
                    if not to_acc:
                        pe.sem_inc(s_u, CREDIT)

                    def turn(b, par, n):
                        pe.wait_ge(s_stage, done(b))
                        pe.wait_ge(s_dve, done(b - 2))
                        for k in range(n):
                            last = nc.tensor.transpose(pt[par][:, k * P:(k + 1) * P],
                                                       staged[:, par, k * P:(k + 1) * P], ident[:, :])
                        last.then_inc(s_pe, 1)

                    def product(b, par, n):
                        if not to_acc:
                            pe.wait_ge(s_dve, done(b))
                            pe.wait_ge(s_act, done(b - 2))
                            for k in range(n):
                                last = nc.tensor.matmul(pu[par][:, k * P:k * P + width],
                                                        turned[:, par, k * P:(k + 1) * P], weight,
                                                        start=True, stop=True)
                            last.then_inc(s_u, 1)
                    turn(0, 0, TB)
                    with pe.Fori(0, FULLS // 2 - 1) as q:
                        turn(2 * q + 1, 1, TB)
                        product(2 * q, 0, TB)
                        turn(2 * q + 2, 0, TB)
                        product(2 * q + 1, 1, TB)
                    turn(FULLS - 1, 1, TB)
                    product(FULLS - 2, 0, TB)
                    for b, n in tails:
                        turn(b, b % 2, n)
                    product(FULLS - 1, 1, TB)
                    for b, n in tails:
                        product(b, b % 2, n)

                @block.vector
                def _(dve):
                    dve.sem_inc(s_dve, CREDIT)

                    def one(b, par, n):
                        dve.wait_ge(s_pe, done(b))
                        if to_acc:
                            nc.vector.tensor_copy(
                                acc[:, 0:NPAD].rearrange("f (p t) -> f t p", t=NT)[:, ds(b * TB, n), :],
                                slots(pt[par], n)).then_inc(s_dve, 1)
                        else:
                            dve.wait_ge(s_u, done(b - 2))
                            nc.vector.tensor_copy(turned[:, par, 0:n * P], pt[par][:, 0:n * P]).then_inc(s_dve, 1)
                    with dve.Fori(0, FULLS // 2) as q:
                        one(2 * q, 0, TB)
                        one(2 * q + 1, 1, TB)
                    for b, n in tails:
                        one(b, b % 2, n)

                @block.scalar
                def _(act):
                    act.sem_inc(s_act, CREDIT)
                    act.sem_inc(s_stage, CREDIT)
                    act.preload_act_table(ACT.Copy)

                    def fetch(b, par, n):
                        act.wait_ge(s_pe, done(b - 2))
                        act.nop(nofuse=True)
                        nc.scalar.activation(slots(staged[:, par, :], n), source[:, ds(b * TB, n), :],
                                             ACT.Copy).then_inc(s_stage, 1)

                    def take(b, par, n):
                        if not to_acc:
                            act.wait_ge(s_u, done(b))
                            act.nop(nofuse=True)
                            nc.scalar.activation(into[:, ds(b * TB, n), 0:width],
                                                 slots(pu[par], n)[:, :, 0:width], ACT.Copy).then_inc(s_act, 1)
                    fetch(0, 0, TB)
                    fetch(1, 1, TB)
                    with act.Fori(0, FULLS // 2 - 1) as q:
                        fetch(2 * q + 2, 0, TB)
                        take(2 * q, 0, TB)
                        fetch(2 * q + 3, 1, TB)
                        take(2 * q + 1, 1, TB)
                    for b, n in tails:
                        fetch(b, b % 2, n)
                    take(FULLS - 2, 0, TB)
                    take(FULLS - 1, 1, TB)
                    for b, n in tails:
                        take(b, b % 2, n)
            end_stage()

        def project_acc(weight, into):
            with nc.Block() as block:
                @block.tensor
                def _(pe):
                    pe.sem_inc(s_pe, CREDIT)

                    def one(t, par):
                        pe.wait_ge(s_stage, done(t))
                        pe.wait_ge(s_act, done(t - 2))
                        nc.tensor.matmul(pt[par][:, 0:D], stage[:, par, :], weight, start=True,
                                         stop=True).then_inc(s_pe, 1)
                    with pe.Fori(0, NT // 2) as q:
                        one(2 * q, 0)
                        one(2 * q + 1, 1)
                    for t in range(NT // 2 * 2, NT):
                        one(t, t % 2)

                @block.vector
                def _(dve):
                    dve.sem_inc(s_stage, CREDIT)

                    def one(t, par):
                        dve.wait_ge(s_pe, done(t - 2))
                        nc.vector.tensor_copy(stage[:, par, :].unsqueeze(1),
                                              acc[:, 0:NPAD].rearrange("f (p t) -> f t p", t=NT)[:, ds(t, 1), :]
                                              ).then_inc(s_stage, 1)
                    with dve.Fori(0, NT // 2) as q:
                        one(2 * q, 0)
                        one(2 * q + 1, 1)
                    for t in range(NT // 2 * 2, NT):
                        one(t, t % 2)

                @block.scalar
                def _(act):
                    act.sem_inc(s_act, CREDIT)
                    act.preload_act_table(ACT.Copy)

                    def one(t, par):
                        act.wait_ge(s_pe, done(t))
                        act.nop(nofuse=True)
                        nc.scalar.activation(into[:, ds(t, 1), :], pt[par][:, 0:D].unsqueeze(1),
                                             ACT.Copy).then_inc(s_act, 1)
                    with act.Fori(0, NT // 2) as q:
                        one(2 * q, 0)
                        one(2 * q + 1, 1)
                    for t in range(NT // 2 * 2, NT):
                        one(t, t % 2)
            end_stage()

        def store_tables(*pairs):
            with nc.Block() as block:
                @block.sync
                def _(sp):
                    for d_, s_ in pairs:
                        sp.dma_start(d_.rearrange("(p t) f -> p t f", t=NT), s_).then_inc(s_store, 16)
                    sp.wait_ge(s_store, 16 * len(pairs))
            end_stage()

        def degrees():
            with nc.Block() as block:
                @block.sync
                def _(sp):
                    sp.dma_start(deg_d, acc[0:2, 0:NPAD]).then_inc(s_store, 16)
                    sp.wait_ge(s_store, 16)
                    for r_, d_ in ((0, dinv), (1, cinv)):
                        sp.dma_start(d_[:, :], deg_d[r_, :].rearrange("(p t) -> p t", t=NT)).then_inc(s_load, 16)
                    sp.wait_ge(s_load, 32)

                @block.vector
                def _(dve):
                    link = chain(dve, s_dve)
                    dve.wait_ge(s_load, 32)
                    link(nc.vector.tensor_scalar(cinv[:, :], cinv[:, :], 1.0, None, ALU.max))
                    link(nc.vector.reciprocal(cinv[:, :], cinv[:, :]))
                    dve.wait_ge(s_act, 1)
                    link(nc.vector.reciprocal(dinv[:, :], dinv[:, :]))
                    link(nc.vector.tensor_copy(dinv3[:, 0, :], dinv[:, :]))
                    link(nc.vector.tensor_tensor(drest[:, 0, :], dinv[:, :], dinv3[:, 0, :], ALU.subtract))
                    link(nc.vector.tensor_copy(dinv3[:, 1, :], drest[:, 0, :]))
                    link(nc.vector.tensor_tensor(drest[:, 1, :], drest[:, 0, :], dinv3[:, 1, :], ALU.subtract))
                    link(nc.vector.tensor_copy(dinv3[:, 2, :], drest[:, 1, :]))
                    link(nc.vector.tensor_tensor(big, h_sb[:, :, :], bc_t(dinv), ALU.mult))

                @block.scalar
                def _(act):
                    act.wait_ge(s_load, 32)
                    nc.scalar.activation(dinv[:, :], dinv[:, :], ACT.Sqrt, bias=1.0).then_inc(s_act, 1)
            end_stage()

        def gcn(weight, bias, gain, shift):
            degrees()
            transpose_project(big, to_acc=True)
            reset_windows()
            with nc.Fori(0, rounds):
                sum_kept_round()
            project_acc(weight, h_sb)
            with nc.Block() as block:
                @block.vector
                def _(dve):
                    link = chain(dve, s_dve)
                    link(nc.vector.tensor_tensor(h_sb[:, :, :], h_sb[:, :, :], bc_t(dinv), ALU.mult))
                    link(nc.vector.tensor_tensor(h_sb[:, :, :], h_sb[:, :, :], bc_f(bias), ALU.add))

                @block.scalar
                def _(act):
                    act.wait_ge(s_dve, 2)
                    nc.scalar.activation(h_sb[:, :, :], h_sb[:, :, :], ACT.Gelu).then_inc(s_act, 1)
            end_stage()

        with nc.Block() as block:
            @block.vector
            def _(dve):
                nc.vector.tensor_scalar(hsgw[:, :], sgw[:, 0:1], 0.5, None, ALU.mult)
                nc.vector.tensor_copy(h_sb[:, :, :], x_sb[:, :, :])
        end_stage()
        H = h_sb[:, :, :]
        layernorm(H, big, relu_to=H)
        transpose_project(h_sb, w_pq[:, :], into=big)
        store_tables((tab_p[:, ED:ED + D], H), (tab_q[0:NPAD, :], big[:, :, ED:2 * ED]),
                     (tab_pr[:, 0:ED], big[:, :, 0:ED]), (tab_qs[0:NPAD, 0:ED], big[:, :, ED:2 * ED]))
        with nc.Block() as block:
            @block.vector
            def _(dve):
                nc.vector.tensor_tensor(big[:, :, 0:ED], big[:, :, 0:ED],
                                        eib1_row[:, :].unsqueeze(1).broadcast_to([P, NT, ED]), ALU.add)
        end_stage()
        store_tables((tab_p[:, 0:ED], big[:, :, 0:ED]))
        reset_windows(clear_weights=True, clear_rows=2)
        with nc.Fori(0, rounds):
            edge_round(False)
        gcn(w1[:, :], 0, 2, 3)
        layernorm(H, big, gain=2, shift=3)
        transpose_project(h_sb, u1[:, :], into=big)
        store_tables((tab_pr[:, ED:PR], big), (tab_pr[:, PR:PR + D], H))
        transpose_project(h_sb, u2[:, :], into=big)
        store_tables((tab_qs[0:NPAD, ED:PR], big))
        reset_windows(clear_weights=True, clear_rows=2)
        with nc.Fori(0, rounds):
            edge_round(True)
        gcn(w2[:, :], 1, 4, 5)
        layernorm(H, big, gain=4, shift=5, add_to=x_sb[:, :, :])
        layernorm(H, big, before=[lambda: nc.vector.tensor_copy(H, x_sb[:, :, :])], relu_to=H)

        store_tables((tab_h, H))
        reset_windows(clear_rows=P)
        with nc.Fori(0, rounds):
            sum_round()
        project_acc(l1b[:, :], big)
        with nc.Block() as block:
            @block.vector
            def _(dve):
                link = chain(dve, s_dve)
                link(nc.vector.tensor_tensor(big, big, bc_t(cinv), ALU.mult))
                link(nc.vector.tensor_tensor(big, big, bc_f(6), ALU.add))
        end_stage()
        transpose_project(h_sb, l1a[:, :], into=h_sb)
        with nc.Block() as block:
            @block.vector
            def _(dve):
                link = chain(dve, s_dve)
                link(nc.vector.tensor_tensor(big, big, H, ALU.add))
                link(nc.vector.tensor_tensor(H, big, big, ALU.mult))
                link(nc.vector.tensor_reduce(s1[:, :], H, axis=AXX, op=ALU.add))
                dve.wait_ge(s_act, 1)
                link(nc.vector.tensor_scalar(s1[:, :], s1[:, :], 1e-12, None, ALU.max))
                link(nc.vector.reciprocal(s1[:, :], s1[:, :]))
                link(nc.vector.tensor_tensor(big, big, bc_t(s1), ALU.mult))
                link(nc.vector.scalar_tensor_tensor(x_sb[:, :, :], big, 0.0, x_sb[:, :, :], ALU.max, ALU.add))

            @block.scalar
            def _(act):
                act.wait_ge(s_dve, 3)
                nc.scalar.activation(s1[:, :], s1[:, :], ACT.Sqrt).then_inc(s_act, 1)

            @block.sync
            def _(sp):
                sp.wait_ge(s_dve, 7)
                sp.dma_start(out[0:FULL * NT, :].rearrange("(p t) d -> p t d", t=NT),
                             x_sb[0:FULL, :, :]).then_inc(s_store, 16)
                sp.dma_start(out[FULL * NT:N, :].rearrange("(p t) d -> p t d", p=1),
                             x_sb[FULL:FULL + 1, 0:REST, :]).then_inc(s_store, 16)
                sp.wait_ge(s_store, 32)


_INS = ["x", "src", "dst", "L0_gnn_W1", "L0_gnn_b1", "L0_gnn_W2", "L0_gnn_b2", "L0_gnn_ln1_g", "L0_gnn_ln1_b",
        "L0_gnn_ln2_g", "L0_gnn_ln2_b", "L0_gnn_ei_w1", "L0_gnn_ei_b1", "L0_gnn_ei_w2", "L0_gnn_ei_b2",
        "L0_gnn_eu_w1", "L0_gnn_eu_b1", "L0_gnn_eu_w2", "L0_gnn_eu_b2", "L0_gnn_lne_g", "L0_gnn_lne_b",
        "L0_gnn_ew_w", "L0_gnn_ew_b", "L1_gnn_W", "L1_gnn_b"]


def kernel(**inputs):
    import numpy as _np
    import concourse.bacc as _bacc
    from concourse import mybir as _mybir
    from concourse.bass_utils import run_bass_kernel_spmd as _run

    nc = _bacc.Bacc("TRN2", target_bir_lowering=False, num_devices=1)
    arrays, args = {}, []
    for name in _INS:
        a = _np.ascontiguousarray(inputs[name])
        arrays[f"in_{name}_dram"] = a
        args.append(nc.dram_tensor(f"in_{name}_dram", a.shape, _mybir.dt.from_np(a.dtype), kind="ExternalInput").ap())
    args.append(nc.dram_tensor("out_dram", inputs["x"].shape, _mybir.dt.float32, kind="ExternalOutput").ap())
    build(nc, *args)
    r = _run(nc, [arrays], core_ids=[0])
    return r.results[0]["out_dram"]
```
